# Optimizing a Trainium2 kernel written in Bass

```python
import numpy as np
import jax
import jax.numpy as jnp

def _softmax(x, axis=-1):
    return jax.nn.softmax(x, axis=axis)

def _gelu(x):
    return jax.nn.gelu(x, approximate=True)

def _silu(x):
    return jax.nn.silu(x)

def _sigmoid(x):
    return jax.nn.sigmoid(x)

def _layernorm(x, axis=-1, eps=1e-05):
    m = jnp.mean(x, axis=axis, keepdims=True)
    v = jnp.var(x, axis=axis, keepdims=True)
    return (x - m) / jnp.sqrt(v + eps)

def _scatter_add(tgt, idx, src, axis=0):
    return tgt.at[idx].add(src)

def _segment_sum(src, seg, n):
    return jax.ops.segment_sum(src, seg, n)
kernel_name = 'mk_gnn_resnorm_d4_gnn_r32_ba1c04'

def setup_inputs(seed: int=0):
    np.random.seed(seed)
    _w = jnp.asarray

    def _rec_inputs():
        import jax
        import jax.numpy as jnp
        _gk = jax.random.key(seed)
        x = -0.0005121 + 1.001 * jax.random.normal(jax.random.fold_in(_gk, 1), (3125, 16), jnp.float32)
        _s = jax.random.randint(jax.random.fold_in(_gk, 2), (50000,), 0, 3125, jnp.int32)
        _d = jax.random.randint(jax.random.fold_in(_gk, 3), (50000,), 0, 3125, jnp.int32)
        _loop = jnp.arange(3125, dtype=jnp.int32)
        src = jnp.concatenate([_s, _d, _loop])
        dst = jnp.concatenate([_d, _s, _loop])
        _o = jnp.argsort(dst, stable=True)
        src = src[_o]
        dst = dst[_o]
        edge_attr_16 = -0.00010739 + 0.99994 * jax.random.normal(jax.random.fold_in(_gk, 12), (103125, 16), jnp.float32)
        edge_attr_4 = 0.000714719 + 1.00021 * jax.random.normal(jax.random.fold_in(_gk, 13), (103125, 4), jnp.float32)
        edge_type_8 = jax.random.randint(jax.random.fold_in(_gk, 15), (103125,), 0, 8, jnp.int32)
        edge_type_90 = jax.random.randint(jax.random.fold_in(_gk, 16), (103125,), 0, 90, jnp.int32)
        edge_weight1 = jax.random.uniform(jax.random.fold_in(_gk, 17), (103125, 1), jnp.float32, 0.0, 1)
        node_vec1 = jax.random.uniform(jax.random.fold_in(_gk, 18), (3125, 1), jnp.float32, 0.0, 1)
        return (x, src, dst, edge_attr_16, edge_attr_4, edge_type_8, edge_type_90, edge_weight1, node_vec1)
    x, src, dst, edge_attr_16, edge_attr_4, edge_type_8, edge_type_90, edge_weight1, node_vec1 = _rec_inputs()

    def _L0_gnn_setup():
        import jax, jax.numpy as jnp
        import numpy as np
        N_NODES = 6250
        N_EDGES = 100000
        F_IN = 16
        N_CLASSES = 16

        def _gin_conv(x, src, dst, eps, wa, ba, wb, bb, n_nodes):
            agg = jax.ops.segment_sum(x[src], dst, num_segments=n_nodes)
            h = (1.0 + eps) * x + agg
            h = jax.nn.relu(h @ wa + ba) @ wb + bb
            return h
        key = jax.random.key(seed)
        ks = jax.random.split(key, 8)
        s = 1.0 / np.sqrt(F_IN)
        return {'x': jax.random.normal(ks[0], (N_NODES, F_IN), dtype=jnp.float32), 'edge_index': jax.random.randint(ks[1], (2, N_EDGES), 0, N_NODES, dtype=jnp.int32), 'eps1': jnp.zeros((), dtype=jnp.float32), 'w1a': jax.random.normal(ks[2], (F_IN, 16), dtype=jnp.float32) * s, 'b1a': jnp.zeros((16,), dtype=jnp.float32), 'w1b': jax.random.normal(ks[3], (16, 16), dtype=jnp.float32) * 0.25, 'b1b': jnp.zeros((16,), dtype=jnp.float32), 'eps2': jnp.zeros((), dtype=jnp.float32), 'w2a': jax.random.normal(ks[4], (16, N_CLASSES), dtype=jnp.float32) * 0.25, 'b2a': jnp.zeros((N_CLASSES,), dtype=jnp.float32), 'w2b': jax.random.normal(ks[5], (N_CLASSES, N_CLASSES), dtype=jnp.float32) * 0.25, 'b2b': jnp.zeros((N_CLASSES,), dtype=jnp.float32)}
    _L0_gnn_all = _L0_gnn_setup()
    _L0_gnn_in = {k: v for k, v in _L0_gnn_all.items() if k in ('eps1', 'w1a', 'b1a', 'w1b', 'b1b', 'eps2', 'w2a', 'b2a', 'w2b', 'b2b')}
    del _L0_gnn_all

    def _L1_gnn_setup():
        import jax, jax.numpy as jnp
        import numpy as np
        N, E = (50000, 25000)
        IN_NF, EDGE_NF, HID, OUT_NF, L = (16, 4, 128, 16, 4)

        def _lin(key, fan_in, fan_out):
            kw, kb = jax.random.split(key)
            bound = 1.0 / np.sqrt(fan_in)
            w = jax.random.uniform(kw, (fan_in, fan_out), jnp.float32, -bound, bound)
            b = jax.random.uniform(kb, (fan_out,), jnp.float32, -bound, bound)
            return (w, b)
        key = jax.random.key(seed)
        ks = jax.random.split(key, 16)
        h = jax.random.normal(ks[0], (N, IN_NF), jnp.float32)
        edge_index = jax.random.randint(ks[1], (2, E), 0, N, jnp.int32)
        edge_attr = jax.random.normal(ks[2], (E, EDGE_NF), jnp.float32)
        node_mask = jnp.ones((N, 1), jnp.float32)
        edge_mask = jnp.ones((E, 1), jnp.float32)
        emb_w, emb_b = _lin(ks[3], IN_NF, HID)
        out_w, out_b = _lin(ks[4], HID, OUT_NF)
        e1 = [_lin(jax.random.fold_in(ks[5], i), 2 * HID + EDGE_NF, HID) for i in range(L)]
        e2 = [_lin(jax.random.fold_in(ks[6], i), HID, HID) for i in range(L)]
        n1 = [_lin(jax.random.fold_in(ks[7], i), 2 * HID, HID) for i in range(L)]
        n2 = [_lin(jax.random.fold_in(ks[8], i), HID, HID) for i in range(L)]
        stk = lambda ps, j: jnp.stack([p[j] for p in ps])
        return {'h': h, 'edge_index': edge_index, 'edge_attr': edge_attr, 'node_mask': node_mask, 'edge_mask': edge_mask, 'emb_w': emb_w, 'emb_b': emb_b, 'edge_w1': stk(e1, 0), 'edge_b1': stk(e1, 1), 'edge_w2': stk(e2, 0), 'edge_b2': stk(e2, 1), 'node_w1': stk(n1, 0), 'node_b1': stk(n1, 1), 'node_w2': stk(n2, 0), 'node_b2': stk(n2, 1), 'out_w': out_w, 'out_b': out_b}
    _L1_gnn_all = _L1_gnn_setup()
    _L1_gnn_in = {k: v for k, v in _L1_gnn_all.items() if k in ('emb_w', 'emb_b', 'edge_w1', 'edge_b1', 'edge_w2', 'edge_b2', 'node_w1', 'node_b1', 'node_w2', 'node_b2', 'out_w', 'out_b')}
    del _L1_gnn_all

    def _L2_gnn_setup():
        import jax, jax.numpy as jnp
        import numpy as np
        N, E, IN, OUT, R, B = (50000, 25000, 16, 16, 90, 30)
        key = jax.random.key(seed)
        ks = jax.random.split(key, 9)
        h = jax.random.normal(ks[0], (N, IN), dtype=jnp.float32)
        he = jax.random.normal(ks[1], (E, IN), dtype=jnp.float32)
        Ws = jax.random.normal(ks[2], (OUT, IN), dtype=jnp.float32) * 0.1
        Wa = jax.random.normal(ks[3], (1, 3 * OUT), dtype=jnp.float32) * 0.1
        weight = jax.random.normal(ks[4], (B, IN, OUT), dtype=jnp.float32) * 0.1
        w_comp = jax.random.normal(ks[5], (R, B), dtype=jnp.float32) * 0.1
        src = jax.random.randint(ks[6], (E,), 0, N)
        dst = jax.random.randint(ks[7], (E,), 0, N)
        rel_type = jax.random.randint(ks[8], (E,), 0, R)
        return {'h': h, 'he': he, 'Ws': Ws, 'Wa': Wa, 'weight': weight, 'w_comp': w_comp, 'src': src, 'dst': dst, 'rel_type': rel_type}
    _L2_gnn_all = _L2_gnn_setup()
    _L2_gnn_in = {k: v for k, v in _L2_gnn_all.items() if k in ('Ws', 'Wa', 'weight', 'w_comp')}
    del _L2_gnn_all

    def _L3_gnn_setup():
        import jax, jax.numpy as jnp
        import numpy as np
        N_NODES = 3125
        N_EDGES = 100000
        NUM_REL = 8

        def _rgcn_layer(x, src, dst, edge_type, W, root, bias):
            out = x @ root + bias
            x_src = x[src]
            for r in range(W.shape[0]):
                mask = (edge_type == r).astype(x.dtype)
                s = jax.ops.segment_sum(x_src * mask[:, None], dst, num_segments=x.shape[0])
                cnt = jax.ops.segment_sum(mask, dst, num_segments=x.shape[0])
                agg = s / jnp.clip(cnt, 1.0)[:, None]
                out = out + agg @ W[r]
            return out
        key = jax.random.key(seed)
        ks = jax.random.split(key, 9)
        x = jax.random.normal(ks[0], (N_NODES, 16), dtype=jnp.float32)
        edge_index = jax.random.randint(ks[1], (2, N_EDGES), 0, N_NODES, dtype=jnp.int32)
        edge_type = jax.random.randint(ks[2], (N_EDGES,), 0, NUM_REL, dtype=jnp.int32)
        s1 = 1.0 / np.sqrt(16.0)
        s2 = 1.0 / np.sqrt(32.0)
        W1 = jax.random.normal(ks[3], (NUM_REL, 16, 32), dtype=jnp.float32) * s1
        root1 = jax.random.normal(ks[4], (16, 32), dtype=jnp.float32) * s1
        b1 = jnp.zeros((32,), dtype=jnp.float32)
        W2 = jax.random.normal(ks[5], (NUM_REL, 32, 16), dtype=jnp.float32) * s2
        root2 = jax.random.normal(ks[6], (32, 16), dtype=jnp.float32) * s2
        b2 = jnp.zeros((16,), dtype=jnp.float32)
        return {'x': x, 'edge_index': edge_index, 'edge_type': edge_type, 'W1': W1, 'root1': root1, 'b1': b1, 'W2': W2, 'root2': root2, 'b2': b2}
    _L3_gnn_all = _L3_gnn_setup()
    _L3_gnn_in = {k: v for k, v in _L3_gnn_all.items() if k in ('W1', 'root1', 'b1', 'W2', 'root2', 'b2')}
    del _L3_gnn_all
    return {'x': x, 'src': src, 'dst': dst, 'edge_attr_16': edge_attr_16, 'edge_attr_4': edge_attr_4, 'edge_type_8': edge_type_8, 'edge_type_90': edge_type_90, 'edge_weight1': edge_weight1, 'node_vec1': node_vec1, 'L0_gnn_eps1': _L0_gnn_in['eps1'], 'L0_gnn_w1a': _L0_gnn_in['w1a'], 'L0_gnn_b1a': _L0_gnn_in['b1a'], 'L0_gnn_w1b': _L0_gnn_in['w1b'], 'L0_gnn_b1b': _L0_gnn_in['b1b'], 'L0_gnn_eps2': _L0_gnn_in['eps2'], 'L0_gnn_w2a': _L0_gnn_in['w2a'], 'L0_gnn_b2a': _L0_gnn_in['b2a'], 'L0_gnn_w2b': _L0_gnn_in['w2b'], 'L0_gnn_b2b': _L0_gnn_in['b2b'], 'L1_gnn_emb_w': _L1_gnn_in['emb_w'], 'L1_gnn_emb_b': _L1_gnn_in['emb_b'], 'L1_gnn_edge_w1': _L1_gnn_in['edge_w1'], 'L1_gnn_edge_b1': _L1_gnn_in['edge_b1'], 'L1_gnn_edge_w2': _L1_gnn_in['edge_w2'], 'L1_gnn_edge_b2': _L1_gnn_in['edge_b2'], 'L1_gnn_node_w1': _L1_gnn_in['node_w1'], 'L1_gnn_node_b1': _L1_gnn_in['node_b1'], 'L1_gnn_node_w2': _L1_gnn_in['node_w2'], 'L1_gnn_node_b2': _L1_gnn_in['node_b2'], 'L1_gnn_out_w': _L1_gnn_in['out_w'], 'L1_gnn_out_b': _L1_gnn_in['out_b'], 'L2_gnn_Ws': _L2_gnn_in['Ws'], 'L2_gnn_Wa': _L2_gnn_in['Wa'], 'L2_gnn_weight': _L2_gnn_in['weight'], 'L2_gnn_w_comp': _L2_gnn_in['w_comp'], 'L3_gnn_W1': _L3_gnn_in['W1'], 'L3_gnn_root1': _L3_gnn_in['root1'], 'L3_gnn_b1': _L3_gnn_in['b1'], 'L3_gnn_W2': _L3_gnn_in['W2'], 'L3_gnn_root2': _L3_gnn_in['root2'], 'L3_gnn_b2': _L3_gnn_in['b2']}

def reference(x, src, dst, edge_attr_16, edge_attr_4, edge_type_8, edge_type_90, edge_weight1, node_vec1, L0_gnn_eps1, L0_gnn_w1a, L0_gnn_b1a, L0_gnn_w1b, L0_gnn_b1b, L0_gnn_eps2, L0_gnn_w2a, L0_gnn_b2a, L0_gnn_w2b, L0_gnn_b2b, L1_gnn_emb_w, L1_gnn_emb_b, L1_gnn_edge_w1, L1_gnn_edge_b1, L1_gnn_edge_w2, L1_gnn_edge_b2, L1_gnn_node_w1, L1_gnn_node_b1, L1_gnn_node_w2, L1_gnn_node_b2, L1_gnn_out_w, L1_gnn_out_b, L2_gnn_Ws, L2_gnn_Wa, L2_gnn_weight, L2_gnn_w_comp, L3_gnn_W1, L3_gnn_root1, L3_gnn_b1, L3_gnn_W2, L3_gnn_root2, L3_gnn_b2):
    import jax
    import jax.numpy as jnp

    def _L0_gnn_ref(x, edge_index, eps1, w1a, b1a, w1b, b1b, eps2, w2a, b2a, w2b, b2b):
        import jax, jax.numpy as jnp
        import numpy as np
        N_NODES = 6250
        N_EDGES = 100000
        F_IN = 16
        N_CLASSES = 16

        def _gin_conv(x, src, dst, eps, wa, ba, wb, bb, n_nodes):
            agg = jax.ops.segment_sum(x[src], dst, num_segments=n_nodes)
            h = (1.0 + eps) * x + agg
            h = jax.nn.relu(h @ wa + ba) @ wb + bb
            return h
        src, dst = (edge_index[0], edge_index[1])
        n = x.shape[0]
        h = jax.nn.relu(_gin_conv(x, src, dst, eps1, w1a, b1a, w1b, b1b, n))
        h = _gin_conv(h, src, dst, eps2, w2a, b2a, w2b, b2b, n)
        return jax.nn.log_softmax(h, axis=1)

    def _L1_gnn_ref(h, edge_index, edge_attr, node_mask, edge_mask, emb_w, emb_b, edge_w1, edge_b1, edge_w2, edge_b2, node_w1, node_b1, node_w2, node_b2, out_w, out_b):
        import jax, jax.numpy as jnp
        import numpy as np
        N, E = (50000, 25000)
        IN_NF, EDGE_NF, HID, OUT_NF, L = (16, 4, 128, 16, 4)

        def _lin(key, fan_in, fan_out):
            kw, kb = jax.random.split(key)
            bound = 1.0 / np.sqrt(fan_in)
            w = jax.random.uniform(kw, (fan_in, fan_out), jnp.float32, -bound, bound)
            b = jax.random.uniform(kb, (fan_out,), jnp.float32, -bound, bound)
            return (w, b)
        row, col = (edge_index[0], edge_index[1])
        n = h.shape[0]
        h = h @ emb_w + emb_b
        for i in range(L):
            ef = jnp.concatenate([h[row], h[col], edge_attr], axis=1)
            ef = jax.nn.silu(ef @ edge_w1[i] + edge_b1[i])
            ef = jax.nn.silu(ef @ edge_w2[i] + edge_b2[i])
            ef = ef * edge_mask
            agg = jax.ops.segment_sum(ef, row, num_segments=n)
            nf = jnp.concatenate([h, agg], axis=1)
            nf = jax.nn.silu(nf @ node_w1[i] + node_b1[i])
            nf = nf @ node_w2[i] + node_b2[i]
            h = (h + nf) * node_mask
        out = (h @ out_w + out_b) * node_mask
        return out

    def _L2_gnn_ref(h, he, Ws, Wa, weight, w_comp, src, dst, rel_type):
        import jax, jax.numpy as jnp
        import numpy as np
        N, E, IN, OUT, R, B = (50000, 25000, 16, 16, 90, 30)
        n_nodes, in_dim = h.shape
        num_bases, _, out_dim = weight.shape
        num_rels = w_comp.shape[0]
        V = weight.reshape(in_dim, num_bases, out_dim)
        W_rel = jnp.matmul(w_comp, V).reshape(num_rels, in_dim, out_dim)
        h_src = h[src]
        z_src = h_src @ Ws.T
        z_dst = h[dst] @ Ws.T
        z_e = he @ Ws.T
        e = jnp.concatenate([z_src, z_e, z_dst], axis=1) @ Wa.T
        msg = jnp.einsum('ei,eio->eo', h_src, W_rel[rel_type]) * e
        h_out = jax.ops.segment_sum(msg, dst, num_segments=n_nodes)
        return h_out

    def _L3_gnn_ref(x, edge_index, edge_type, W1, root1, b1, W2, root2, b2):
        import jax, jax.numpy as jnp
        import numpy as np
        N_NODES = 3125
        N_EDGES = 100000
        NUM_REL = 8

        def _rgcn_layer(x, src, dst, edge_type, W, root, bias):
            out = x @ root + bias
            x_src = x[src]
            for r in range(W.shape[0]):
                mask = (edge_type == r).astype(x.dtype)
                s = jax.ops.segment_sum(x_src * mask[:, None], dst, num_segments=x.shape[0])
                cnt = jax.ops.segment_sum(mask, dst, num_segments=x.shape[0])
                agg = s / jnp.clip(cnt, 1.0)[:, None]
                out = out + agg @ W[r]
            return out
        src, dst = (edge_index[0], edge_index[1])
        h = _rgcn_layer(x, src, dst, edge_type, W1, root1, b1)
        h = jax.nn.relu(h)
        h = _rgcn_layer(h, src, dst, edge_type, W2, root2, b2)
        return h
    edge_index = jnp.stack([src, dst])
    x = _layernorm(x + _L0_gnn_ref(x, edge_index, L0_gnn_eps1, L0_gnn_w1a, L0_gnn_b1a, L0_gnn_w1b, L0_gnn_b1b, L0_gnn_eps2, L0_gnn_w2a, L0_gnn_b2a, L0_gnn_w2b, L0_gnn_b2b), axis=-1)
    x = _layernorm(x + _L1_gnn_ref(x, edge_index, edge_attr_4, node_vec1, edge_weight1, L1_gnn_emb_w, L1_gnn_emb_b, L1_gnn_edge_w1, L1_gnn_edge_b1, L1_gnn_edge_w2, L1_gnn_edge_b2, L1_gnn_node_w1, L1_gnn_node_b1, L1_gnn_node_w2, L1_gnn_node_b2, L1_gnn_out_w, L1_gnn_out_b), axis=-1)
    x = _layernorm(x + _L2_gnn_ref(x, edge_attr_16, L2_gnn_Ws, L2_gnn_Wa, L2_gnn_weight, L2_gnn_w_comp, src, dst, edge_type_90), axis=-1)
    x = _layernorm(x + _L3_gnn_ref(x, edge_index, edge_type_8, L3_gnn_W1, L3_gnn_root1, L3_gnn_b1, L3_gnn_W2, L3_gnn_root2, L3_gnn_b2), axis=-1)
    return x

_drawn_inputs = setup_inputs


def setup_inputs(seed=0):
    import zlib

    import numpy as np

    out = dict(_drawn_inputs(seed))
    spreads = {'L0_gnn_b1a': (0.0, 0.8),
     'L0_gnn_b1b': (0.0, 0.479),
     'L0_gnn_b2a': (0.0, 2.0),
     'L0_gnn_b2b': (0.0, 2.0),
     'L3_gnn_b1': (0.0, 0.1),
     'L3_gnn_b2': (0.0, 0.345)}
    factors = {'edge_attr_4': 8.0,
     'edge_weight1': 8.0,
     'L1_gnn_edge_w1': 2.969,
     'L1_gnn_edge_b1': 8.0,
     'L1_gnn_edge_b2': 3.332,
     'L1_gnn_node_b1': 31.537,
     'L1_gnn_node_b2': 2.808,
     'L1_gnn_out_b': 64.0}
    for name, (base, spread) in spreads.items():
        noise = np.random.default_rng([zlib.crc32(name.encode()), seed]).standard_normal(out[name].shape)
        drawn = base * np.exp(spread * noise) if base else spread * noise
        out[name] = jnp.asarray(drawn.astype(out[name].dtype))
    for name, factor in factors.items():
        out[name] = (out[name] * factor).astype(out[name].dtype)
    return out
```

```python
from contextlib import ExitStack

import concourse.bass as bass
from concourse import mybir
from concourse.bass import IndirectOffsetOnAxis

F32 = mybir.dt.float32
I32 = mybir.dt.int32
ALU = mybir.AluOpType
ACT = mybir.ActivationFunctionType
AX = mybir.AxisListType

P = 128
N, FIN = 3125, 16
E = 103125
NB = -(-N // P)
NP = NB * P
G = 4
GE = G * P
NG = E // GE + NB
NG += NG % 2
NT = NG * G
T = -(-E // (P * 8)) * 8
FULL = E // T
TAIL = E - FULL * T
W = 8
HID, L = 128, 4
NREL, NBAS, NTYPE = 90, 30, 8
NOWHERE = 999.0
CH = [(c, min(512, NP - c)) for c in range(0, NP, 512)]
EPS = 1e-5


def gnn_kernel(nc, a, out):
    with ExitStack() as ctx:
        def sb(name, shape, dt=F32, st=None):
            return (st or ctx).enter_context(nc.sbuf_tensor(name, shape, dt))

        def dram(name, shape, dt=F32):
            return nc.dram_tensor(name, shape, dt, kind="Internal").ap()

        def sem(name):
            return ctx.enter_context(nc.semaphore(name))

        class Chain:
            def __init__(self, name):
                self.sem, self.n = sem(name), 0

            def __call__(self, eng, ins, by=1):
                self.n += by
                ins.then_inc(self.sem, by)
                eng.wait_ge(self.sem, self.n)

        class Signal:
            def __init__(self, name):
                self.sem, self.n = sem(name), 0

            def base(self, adds):
                at = self.n
                self.n += adds
                return at

        v_chain, a_chain, p_chain = Chain("v_chain"), Chain("a_chain"), Chain("p_chain")
        sp_dma, pool_dma, act_dma = Chain("sp_dma"), Chain("pool_dma"), Chain("act_dma")
        to_pe, from_pe = Signal("vector_to_pe"), Signal("pe_to_vector")
        to_act, from_act = Signal("vector_to_act"), Signal("act_to_vector")

        gate_open = sem("gate_open")
        gates = [0]

        def gate_before(pool, n):
            if not isinstance(n, int) or n > 0:
                pool.wait_ge(gate_open, n)

        def pool_gate(pool):
            pool.tensor_tensor(pool_cell[:, 1:2], pool_cell[:, 0:1], pool_cell[:, 0:1], ALU.add).then_inc(gate_open, 1)

        list_s = dram("list_by_src", [P * NT + T, W])
        list_d = dram("list_by_dst", [P * NT + T, W])
        rows_s = dram("rows_by_src", [5, NT * P])
        agg_s = dram("agg_by_src", [NG * P, HID])
        agg_d = {w: dram(f"agg_by_dst_{w}", [NG * P, w]) for w in (16, 32, 136, 256)}
        p_tab = dram("p_tab", [NP, HID])
        q_tab = dram("q_tab", [NP, HID])
        x_tab = dram("x_tab", [NP, FIN])
        h_tab = dram("h_tab", [NP, FIN])
        h3_tab = dram("h3_tab", [NP, 32])
        g_tab = dram("g_tab", [FIN * NREL * 16])
        y_tab = dram("y_tab", [NP * NREL, 17])

        pool_cell = sb("pool_cell", [1, 2])
        ident = sb("ident", [P, P])
        iota_row = sb("iota_row", [P, P])
        iota_p = sb("iota_p", [P, 1])
        iota8 = sb("iota8", [P, NTYPE])
        x = sb("x", [P, NB, FIN])
        nodev = sb("nodev", [P, NB])
        tmp = sb("tmp", [P, NB, FIN])
        tmp2 = sb("tmp2", [P, NB, FIN])
        stat = sb("stat", [P, 3, NB])
        epst = sb("epst", [P, 1])
        xT = sb("xT", [FIN, NP])
        col_s = sb("col_s", [P, NT + 2 * G], I32)
        loc_s = sb("loc_s", [P, NT])
        w_s = sb("w_s", [P, NT])
        blk_s = sb("blk_s", [P, NG + 2], I32)
        keep_s = sb("keep_s", [P, NG])
        last_s = sb("last_s", [P, NB], I32)
        src_d = sb("src_d", [P, NT + 2 * G], I32)
        rel_d = sb("rel_d", [P, NT + 2 * G], I32)
        loc_d = sb("loc_d", [P, NT])
        typ_d = sb("typ_d", [P, NT])
        hea_d = sb("hea_d", [P, NT])
        keep_d = sb("keep_d", [P, NG])
        last_d = sb("last_d", [P, NB], I32)
        nrm_d = sb("nrm_d", [P, NB, NTYPE])
        a_rows = sb("a_rows", [P, 2, FIN])
        a_cols = sb("a_cols", [FIN, 3])
        zero_row = sb("zero_row", [P, HID])

        banks = [ctx.enter_context(nc.psum_tensor(f"bank{i}", [P, 512], F32)) for i in range(8)]

        def by_edge(dst, src, lo=0, hi=T):
            pairs, full16 = [], FULL // 16 * 16
            for p0, p1 in ((0, full16), (full16, FULL)):
                v = src[p0 * T:p1 * T]
                v = v.rearrange("(p t) -> p t", t=T) if len(src.shape) == 1 else v.rearrange("(p t) k -> p t k", t=T)
                pairs.append((dst[p0:p1], v[:, lo:hi]))
            n = min(hi, TAIL) - lo
            if n > 0:
                v = src[FULL * T + lo:FULL * T + lo + n]
                v = v.rearrange("(p t) -> p t", p=1) if len(src.shape) == 1 else v.rearrange("(p t) k -> p t k", p=1)
                pairs.append((dst[FULL:FULL + 1, 0:n], v))
            return pairs

        with ExitStack() as st:
            ws = sb("ws", [FIN, FIN], F32, st)
            wa = sb("wa", [FIN, 3], F32, st)
            wab = sb("wab", [FIN, 2, P], F32, st)
            ones16 = sb("ones16", [FIN, P], F32, st)
            b_pe, b_fpe = to_pe.base(1), from_pe.base(1)
            s_init = sem("s_init")
            with nc.Block() as block:
                @block.gpsimd
                def _(pool):
                    p_chain(pool, pool.memset(pool_cell[:, :], 0.0))
                    p_chain(pool, pool.memset(ident[:, :], 0.0))
                    p_chain(pool, pool.affine_select(out=ident[:, :], in_=ident[:, :], compare_op=ALU.not_equal,
                                                     fill=1.0, base=0, pattern=[[-1, P]], channel_multiplier=1))
                    kw = dict(allow_small_or_imprecise_dtypes=True)
                    p_chain(pool, pool.iota(iota_row[:, :], [[1, P]], base=0, channel_multiplier=0, **kw))
                    p_chain(pool, pool.iota(iota_p[:, :], [[0, 1]], base=0, channel_multiplier=1, **kw))
                    p_chain(pool, pool.iota(iota8[:, :], [[1, NTYPE]], base=0, channel_multiplier=0, **kw))

                @block.sync
                def _(sp):
                    sp.wait_ge(s_init, 1)
                    with nc.allow_non_contiguous_dma(reason="small weights"):
                        sp_dma(sp, sp.dma_start(ws[:, :], a["L2_gnn_Ws"]), 16)
                        sp_dma(sp, sp.dma_start(wa[:, :], a["L2_gnn_Wa"].rearrange("a (k o) -> o (a k)", k=3)), 16)
                        full = (N // P) * P
                        sp_dma(sp, sp.dma_start(x[:, 0:N // P, :], a["x"][0:full, :].rearrange("(b p) f -> p b f", p=P)), 16)
                        sp_dma(sp, sp.dma_start(x[0:N - full, NB - 1, :], a["x"][full:N, :]), 16)
                        nv = a["node_vec1"].rearrange("n a -> (n a)")
                        sp_dma(sp, sp.dma_start(nodev[:, 0:N // P], nv[0:full].rearrange("(b p) -> p b", p=P)), 16)
                        sp_dma(sp, sp.dma_start(nodev[0:N - full, NB - 1:NB], nv[full:N].rearrange("(p a) -> p a", a=1)), 16)
                        sp_dma(sp, sp.dma_start(x_tab.rearrange("(b p) f -> p b f", p=P), x[:, :, :]), 16)

                n_dma = sp_dma.n

                @block.vector
                def _(dve):
                    v_chain(dve, dve.memset(x[:, :, :], 0.0))
                    v_chain(dve, dve.memset(zero_row[:, :], 0.0))
                    v_chain(dve, dve.memset(epst[:, :], EPS))
                    v_chain(dve, dve.memset(ones16[:, :], 1.0))
                    dve.memset(nodev[:, :], 0.0).then_inc(s_init, 1)
                    dve.wait_ge(sp_dma.sem, n_dma)
                    v_chain(dve, dve.tensor_scalar(wab[:, 0, :], ones16[:, :], wa[:, 1:2], None, ALU.mult))
                    dve.tensor_scalar(wab[:, 1, :], ones16[:, :], wa[:, 2:3], None, ALU.mult).then_inc(to_pe.sem, 1)
                    dve.wait_ge(from_pe.sem, b_fpe + 1)
                    v_chain(dve, dve.tensor_copy(a_rows[:, :, :], banks[0][:, 0:32].rearrange("p (k i) -> p k i", k=2)))
                    v_chain(dve, dve.tensor_copy(a_cols[:, :], banks[1][0:FIN, 0:3]))

                @block.tensor
                def _(pe):
                    pe.wait_ge(to_pe.sem, b_pe + 1)
                    pe.matmul(banks[0][:, 0:16], wab[:, 0, :], ws[:, :], start=True, stop=True)
                    pe.matmul(banks[0][:, 16:32], wab[:, 1, :], ws[:, :], start=True, stop=True)
                    pe.matmul(banks[1][0:FIN, 0:3], ws[:, :], wa[:, :], start=True, stop=True).then_inc(from_pe.sem, 1)

        with ExitStack() as st:
            srct = sb("srct", [P, T], I32, st)
            dstt = sb("dstt", [P, T], I32, st)
            rec_s = sb("rec_s", [P, T, W], F32, st)
            rec_d = sb("rec_d", [P, T, W], F32, st)
            pos_i = [sb("pos_s", [P, T], I32, st), sb("pos_d", [P, T], I32, st)]
            tri = sb("tri", [P, P], F32, st)
            ones = sb("ones", [P, P], F32, st)
            cnt = sb("cnt", [P, NB], F32, st)
            first = sb("first", [P, NB], F32, st)
            nxt = sb("nxt", [P, NB], F32, st)
            tot = sb("tot", [P, NB], F32, st)
            toti = sb("toti", [P, NB], I32, st)
            delta = sb("delta", [P, NB], F32, st)
            iota_g = sb("iota_g", [P, NG], F32, st)
            accg = sb("accg", [P, NG], F32, st)
            s_load, s_pad, s_cnt, s_tri = sem("s_load"), sem("s_pad"), sem("s_cnt"), sem("s_tri")
            s_const, s_pos, s_ring, s_t8 = sem("s_const"), sem("s_pos"), sem("s_ring"), sem("s_t8")
            scattered = [sem("scattered0"), sem("scattered1")]
            with ExitStack() as st2:
                padt = sb("padt", [P, NT // 8, W], F32, st2)
                ew = sb("ew", [P, T], F32, st2)
                ea4 = sb("ea4", [P, T, 4], F32, st2)
                posf = sb("posf", [P, T], F32, st2)
                ea16 = sb("ea16", [P, T // 4, FIN], F32, st2)
                blkf = sb("blkf", [P, T], F32, st2)
                onehot = sb("onehot", [P, T], F32, st2)
                run = sb("run", [P, T], F32, st2)
                ti = onehot[:, :].bitcast(I32)
                t8 = run[:, :].bitcast(I32)
                s_ea = sem("s_ea")
                s_eafree = sem("s_eafree")
                with nc.Block() as block:
                    @block.gpsimd
                    def _(pool):
                        kw = dict(allow_small_or_imprecise_dtypes=True)
                        p_chain(pool, pool.memset(ones[:, :], 1.0))
                        p_chain(pool, pool.memset(tri[:, :], 1.0))
                        p_chain(pool, pool.affine_select(out=tri[:, :], in_=tri[:, :], compare_op=ALU.is_gt, fill=0.0,
                                                         base=0, pattern=[[1, P]], channel_multiplier=-1))
                        pool.iota(iota_g[:, :], [[1, NG]], base=0, channel_multiplier=0, **kw).then_inc(s_const, 1)

                    @block.sync
                    def _(sp):
                        sp.wait_ge(s_pad, 1)
                        with nc.allow_non_contiguous_dma(reason="records"):
                            for t, v in ((srct, a["src"]), (dstt, a["dst"]), (t8, a["edge_type_8"]), (ti, a["edge_type_90"]),
                                         (ew, a["edge_weight1"].rearrange("e a -> (e a)")), (ea4, a["edge_attr_4"])):
                                for d, v_ in by_edge(t, v):
                                    sp.dma_start(d, v_).then_inc(s_load, 16)
                            for lst in (list_s, list_d):
                                view = lst[0:P * NT, :].rearrange("(p t) w -> p t w", p=P)
                                for c in range(8):
                                    sp.dma_start(view[:, c * (NT // 8):(c + 1) * (NT // 8), :], padt[:, :, :]).then_inc(s_t8, 16)
                            for q in range(4):
                                if q:
                                    sp.wait_ge(s_eafree, q)
                                for d, v_ in by_edge(ea16, a["edge_attr_16"], q * (T // 4), (q + 1) * (T // 4)):
                                    sp.dma_start(d, v_).then_inc(s_ea, 16)
                            sp.wait_ge(s_t8, 256)

                    @block.tensor
                    def _(pe):
                        pe.wait_ge(s_const, 1)
                        for k in range(2):
                            pe.wait_ge(s_cnt, k + 1)
                            pe.matmul(banks[0][:, 0:NB], tri[:, :], cnt[:, :], start=True, stop=True)
                            pe.matmul(banks[1][:, 0:NB], ones[:, :], cnt[:, :], start=True, stop=True).then_inc(s_tri, 1)

                    @block.vector
                    def _(dve):
                        v_chain(dve, dve.memset(padt[:, :, :], 0.0))
                        v_chain(dve, dve.memset(padt[:, :, 0:1], NOWHERE))
                        v_chain(dve, dve.memset(rec_s[:, :, :], 0.0))
                        v_chain(dve, dve.memset(rec_d[:, :, :], 0.0))
                        v_chain(dve, dve.memset(ea16[:, :, :], 0.0))
                        v_chain(dve, dve.memset(ew[:, :], 0.0))
                        v_chain(dve, dve.memset(ea4[:, :, :], 0.0))
                        v_chain(dve, dve.memset(ti, 0))
                        v_chain(dve, dve.memset(t8, 0))
                        v_chain(dve, dve.memset(srct[:, :], 1 << 20))
                        dve.memset(dstt[:, :], 1 << 20).then_inc(s_pad, 1)
                        dve.wait_ge(s_load, 6 * 3 * 16)
                        v_chain(dve, dve.tensor_copy(rec_s[:, :, 2], ew[:, :]))
                        v_chain(dve, dve.tensor_copy(rec_s[:, :, 3:7], ea4[:, :, :]))
                        v_chain(dve, dve.tensor_copy(rec_d[:, :, 3], t8))
                        v_chain(dve, dve.tensor_copy(rec_d[:, :, 1].bitcast(I32), srct[:, :]))
                        v_chain(dve, dve.scalar_tensor_tensor(rec_d[:, :, 2].bitcast(I32), srct[:, :], float(NREL), ti, ALU.mult, ALU.add))
                        v_chain(dve, dve.tensor_copy(rec_s[:, :, 1].bitcast(I32), dstt[:, :]))
                        n_ea = 0
                        for q in range(4):
                            lo, hi = q * (T // 4), (q + 1) * (T // 4)
                            n_ea += 16 * len(by_edge(ea16, a["edge_attr_16"], lo, hi))
                            dve.wait_ge(s_ea, n_ea)
                            v_chain(dve, dve.tensor_tensor(ea16[:, :, :], ea16[:, :, :],
                                                           a_rows[:, 0:1, :].to_broadcast([P, T // 4, FIN]), ALU.mult))
                            dve.tensor_reduce(rec_d[:, lo:hi, 4], ea16[:, :, :], AX.X, ALU.add).then_inc(s_eafree, 1)
                            dve.wait_ge(s_eafree, q + 1)
                        for k, (key, rec, keep, last) in enumerate(((srct, rec_s, keep_s, last_s),
                                                                    (dstt, rec_d, keep_d, last_d))):
                            v_chain(dve, dve.tensor_scalar(ti, key[:, :], P - 1, None, ALU.bitwise_and))
                            v_chain(dve, dve.tensor_copy(rec[:, :, 0], ti))
                            v_chain(dve, dve.tensor_scalar(ti, key[:, :], 7, None, ALU.arith_shift_right))
                            v_chain(dve, dve.tensor_copy(blkf[:, :], ti))
                            for b in range(NB):
                                v_chain(dve, dve.tensor_scalar(onehot[:, :], blkf[:, :], float(b), 0.0, ALU.is_equal,
                                                               ALU.add, accum_out=cnt[:, b:b + 1]))
                            v_chain(dve, dve.tensor_copy(tot[:, :], cnt[:, :]))
                            dve.tensor_copy(first[:, :], cnt[:, :]).then_inc(s_cnt, 1)
                            dve.wait_ge(s_tri, k + 1)
                            v_chain(dve, dve.tensor_scalar(tot[:, :], banks[1][:, 0:NB], float(GE - 1), None, ALU.add))
                            v_chain(dve, dve.tensor_copy(toti[:, :], tot[:, :]))
                            v_chain(dve, dve.tensor_scalar(toti[:, :], toti[:, :], GE.bit_length() - 1, None, ALU.arith_shift_right))
                            v_chain(dve, dve.tensor_copy(tot[:, :], toti[:, :]))
                            v_chain(dve, dve.tensor_scalar(tot[:, :], tot[:, :], 1.0, None, ALU.max))
                            v_chain(dve, dve.tensor_tensor_scan(nxt[:, :], tot[:, :], tot[:, :], 0.0, ALU.add, ALU.bypass))
                            v_chain(dve, dve.tensor_tensor(first[:, :], nxt[:, :], tot[:, :], ALU.subtract))
                            v_chain(dve, dve.tensor_scalar(delta[:, :], first[:, :], float(GE), -1.0, ALU.mult, ALU.add))
                            v_chain(dve, dve.tensor_tensor(delta[:, :], delta[:, :], banks[0][:, 0:NB], ALU.add))
                            v_chain(dve, dve.tensor_scalar(tot[:, :], nxt[:, :], -1.0, float(P), ALU.add, ALU.mult))
                            v_chain(dve, dve.tensor_scalar(last[:, :], tot[:, :], iota_p[:, 0:1], None, ALU.add))
                            dve.wait_ge(s_const, 1)
                            v_chain(dve, dve.memset(accg[:, :], 1.0))
                            for b in range(NB):
                                v_chain(dve, dve.tensor_scalar(keep[:, :], iota_g[:, :], first[:, b:b + 1], -1.0, ALU.is_equal, ALU.mult))
                                v_chain(dve, dve.tensor_tensor(accg[:, :], accg[:, :], keep[:, :], ALU.add))
                            v_chain(dve, dve.tensor_copy(keep[:, :], accg[:, :]))
                            if k == 0:
                                v_chain(dve, dve.memset(accg[:, :], 0.0))
                                for b in range(NB - 1):
                                    v_chain(dve, dve.scalar_tensor_tensor(accg[:, :], iota_g[:, :], nxt[:, b:b + 1], accg[:, :], ALU.is_ge, ALU.add))
                                v_chain(dve, dve.memset(blk_s[:, :], 0))
                                v_chain(dve, dve.tensor_scalar(blk_s[:, 0:NG], accg[:, :], float(P), iota_p[:, 0:1], ALU.mult, ALU.add))
                            v_chain(dve, dve.memset(posf[:, :], -1.0))
                            for b in range(NB):
                                v_chain(dve, dve.tensor_scalar(onehot[:, :], blkf[:, :], float(b), None, ALU.is_equal))
                                v_chain(dve, dve.tensor_tensor_scan(run[:, :], onehot[:, :], onehot[:, :], delta[:, b:b + 1], ALU.add, ALU.bypass))
                                v_chain(dve, dve.copy_predicated(posf[:, :], onehot[:, :].bitcast(I32), run[:, :]))
                            v_chain(dve, dve.tensor_copy(ti, posf[:, :]))
                            v_chain(dve, dve.tensor_scalar(t8, ti, P - 1, None, ALU.bitwise_and))
                            v_chain(dve, dve.tensor_scalar(ti, ti, 7, None, ALU.arith_shift_right))
                            v_chain(dve, dve.scalar_tensor_tensor(pos_i[k][:, :], t8, float(NT), ti, ALU.mult, ALU.add))
                            v_chain(dve, dve.tensor_scalar(onehot[:, :], posf[:, :], 0.0, None, ALU.is_lt))
                            v_chain(dve, dve.memset(run[:, :], 1.0))
                            v_chain(dve, dve.tensor_tensor_scan(run[:, :], run[:, :], run[:, :], float(P * NT - 1), ALU.add, ALU.bypass))
                            v_chain(dve, dve.tensor_copy(t8, run[:, :]))
                            v_chain(dve, dve.copy_predicated(pos_i[k][:, :], onehot[:, :].bitcast(I32), t8))

            ring = sb("ring", [P, 2, 4, W], F32, st)
            rpos = sb("rpos", [P, 2, 4], I32, st)
            ring_ready = sem("ring_ready")
            for k, (rec, lst) in enumerate(((rec_s, list_s), (rec_d, list_d))):
                with nc.Block() as block:
                    @block.vector
                    def _(dve):
                        def fill(i, h, wait):
                            if wait:
                                dve.wait_ge(scattered[h], i * 64 + k * (T // 8) * 64)
                            dve.tensor_copy(ring[:, h, :, :], rec[:, bass.ds(i * 8 + h * 4, 4), :])
                            dve.tensor_copy(rpos[:, h, :], pos_i[k][:, bass.ds(i * 8 + h * 4, 4)]).then_inc(ring_ready, 1)

                        fill(0, 0, k > 0)
                        fill(0, 1, k > 0)
                        with dve.Fori(1, T // 8) as i:
                            fill(i, 0, True)
                            fill(i, 1, True)

                    @block.gpsimd
                    def _(pool):
                        t0 = gates[0]
                        gates[0] += T // 4
                        with pool.Fori(0, T // 8) as i:
                            for h in range(2):
                                gate_before(pool, i * 2 + h + t0)
                                pool.wait_ge(ring_ready, i * 2 + h + 1 + k * (T // 8) * 2)
                                pool_gate(pool)
                                for j in range(4):
                                    pool.indirect_dma_start(lst[:, :], IndirectOffsetOnAxis(ap=rpos[:, h, j:j + 1], axis=0),
                                                            ring[:, h, j, :], None).then_inc(scattered[h], 16)
                        for h in range(2):
                            pool.wait_ge(scattered[h], (k + 1) * (T // 8) * 64)

        with ExitStack() as st:
            lt = sb("lt", [P, NT, W], F32, st)
            rowbuf = sb("rowbuf", [P, 5, 8, P], F32, st)
            s_l, s_take, s_tr, s_cp = sem("s_l"), sem("s_take"), sem("s_tr"), sem("s_cp")
            C8 = NT // 8
            with nc.Block() as block:
                @block.sync
                def _(sp):
                    sp.dma_start(lt[:, :, :].rearrange("p t w -> p (t w)"),
                                 list_s[0:P * NT, :].rearrange("(p t) w -> p (t w)", p=P)).then_inc(s_l, 16)
                    sp.wait_ge(s_take, 1)
                    sp.wait_ge(s_tr, 10)
                    sp.dma_start(lt[:, :, :].rearrange("p t w -> p (t w)"),
                                 list_d[0:P * NT, :].rearrange("(p t) w -> p (t w)", p=P)).then_inc(s_l, 16)
                    sp.wait_ge(s_cp, 10)
                    for r in range(5):
                        sp_dma(sp, sp.dma_start(rows_s[r, :].rearrange("(c t p) -> t c p", c=8, p=P), rowbuf[0:C8, r, :, :]), 16)

                @block.tensor
                def _(pe):
                    pe.wait_ge(s_l, 16)
                    for r in range(5):
                        w = (0, 3, 4, 5, 6)[r]
                        for hf in range(2):
                            n = 2 * r + hf
                            if n >= 2:
                                pe.wait_ge(s_cp, n - 1)
                            for c in range(4):
                                m = pe.transpose(banks[n % 2][0:C8, c * P:(c + 1) * P],
                                                 lt[:, (4 * hf + c) * C8:(4 * hf + c + 1) * C8, w], ident[:, :])
                            m.then_inc(s_tr, 1)

                @block.vector
                def _(dve):
                    dve.memset(col_s[:, NT:], 0)
                    dve.memset(src_d[:, NT:], 0)
                    dve.memset(rel_d[:, NT:], 0)
                    dve.wait_ge(s_l, 16)
                    dve.tensor_copy(loc_s[:, :], lt[:, :, 0])
                    dve.tensor_copy(col_s[:, 0:NT], lt[:, :, 1].bitcast(I32))
                    dve.tensor_copy(w_s[:, :], lt[:, :, 2]).then_inc(s_take, 1)
                    for n in range(10):
                        dve.wait_ge(s_tr, n + 1)
                        dve.tensor_copy(rowbuf[0:C8, n // 2, 4 * (n % 2):4 * (n % 2) + 4, :],
                                        banks[n % 2][0:C8, :].rearrange("t (c p) -> t c p", c=4)).then_inc(s_cp, 1)
                    dve.wait_ge(s_l, 32)
                    dve.tensor_copy(loc_d[:, :], lt[:, :, 0])
                    dve.tensor_copy(src_d[:, 0:NT], lt[:, :, 1].bitcast(I32))
                    dve.tensor_copy(rel_d[:, 0:NT], lt[:, :, 2].bitcast(I32))
                    dve.tensor_copy(typ_d[:, :], lt[:, :, 3])
                    v_chain(dve, dve.tensor_copy(hea_d[:, :], lt[:, :, 4]))

        d_sems = dict(idx=sem("d_idx"), got=[sem("d_got0"), sem("d_got1")], rhs=sem("d_rhs"), sum=sem("d_sum"),
                      acc=sem("d_acc"), stored=[sem("d_stored0"), sem("d_stored1")], taken=sem("d_taken"))
        d_turn = [0]

        def dst_pass(mode, table, idx_all, f, agg):
            width = dict(plain=f, msg=32, types=NTYPE * f + NTYPE, types_only=NTYPE * f)[mode]
            store = agg_d[width]
            typed = mode.startswith("types")
            turn = d_turn[0]
            d_turn[0] += 1
            s, g0, k0 = d_sems, turn * NG, turn * (NG // 2)
            with ExitStack() as st:
                idx = sb(f"idx{turn}", [P, 2, G], I32, st)
                got = sb(f"got{turn}", [P, 2, G, f], F32, st)
                oh = sb(f"oh{turn}", [P, 2, G, P], F32, st)
                rhs = got if mode == "plain" else sb(f"rhs{turn}", [P, 2, G, width], F32, st)
                gate = sb(f"gate{turn}", [P, 2, G], F32, st)
                oh8 = sb(f"oh8{turn}", [P, 2, G, NTYPE], F32, st)
                acc = sb(f"acc{turn}", [P, 2, width], F32, st)
                with nc.Block() as block:
                    @block.gpsimd
                    def _(pool):
                        t0 = gates[0]
                        gates[0] += NG

                        def turn_(k, h, first):
                            gate_before(pool, t0 + k * 2 + h)
                            pool.wait_ge(s["idx"], g0 + k * 2 + h + 1)
                            if not (first and turn == 0):
                                pool.wait_ge(s["sum"] if mode == "plain" else s["rhs"], g0 + k * 2 + h - 1)
                            pool_gate(pool)
                            for j in range(G):
                                pool.indirect_dma_start(got[:, h, j, :], None, table,
                                                        IndirectOffsetOnAxis(ap=idx[:, h, j:j + 1], axis=0)).then_inc(s["got"][h], 16)
                        turn_(0, 0, True)
                        turn_(0, 1, True)
                        with pool.Fori(1, NG // 2) as k:
                            turn_(k, 0, False)
                            turn_(k, 1, False)
                        for h in range(2):
                            pool.wait_ge(s["got"][h], 16 * G * (k0 + NG // 2))
                        for b in range(NB):
                            if b == 0:
                                pool.wait_ge(s["stored"][0], 16 * (k0 + NG // 2))
                                pool.wait_ge(s["stored"][1], 16 * (k0 + NG // 2))
                            pool.indirect_dma_start(agg[:, b, :], None, store,
                                                    IndirectOffsetOnAxis(ap=last_d[:, b:b + 1], axis=0)).then_inc(pool_dma.sem, 16)
                        pool_dma.n += 16 * NB
                        pool.wait_ge(pool_dma.sem, pool_dma.n)

                    @block.sync
                    def _(sp):
                        with sp.Fori(0, NG // 2) as k:
                            for h in range(2):
                                sp.wait_ge(s["acc"], g0 + k * 2 + h + 1)
                                sp.dma_start(store[bass.ds((k * 2 + h) * P, P), :], acc[:, h, :]).then_inc(s["stored"][h], 16)

                    @block.tensor
                    def _(pe):
                        def group(k, h, first):
                            pe.wait_ge(s["rhs"], g0 + k * 2 + h + 1)
                            if mode == "plain":
                                pe.wait_ge(s["got"][h], 16 * G * (k0 + k + 1))
                            if not (first and turn == 0):
                                pe.wait_ge(s["acc"], g0 + k * 2 + h - 1)
                            for j in range(G):
                                m = pe.matmul(banks[h][:, 0:width], oh[:, h, j, :], rhs[:, h, j, :], start=(j == 0), stop=(j == G - 1))
                            m.then_inc(s["sum"], 1)
                        group(0, 0, True)
                        group(0, 1, True)
                        with pe.Fori(1, NG // 2) as k:
                            group(k, 0, False)
                            group(k, 1, False)

                    @block.vector
                    def _(dve):
                        def indices(k, h, first):
                            if not first:
                                dve.wait_ge(s["got"][h], 16 * G * (k0 + k))
                            dve.tensor_copy(idx[:, h, :], idx_all[:, bass.ds((k * 2 + h) * G, G)]).then_inc(s["idx"], 1)

                        def build(k, h, first):
                            if not (first and turn == 0):
                                dve.wait_ge(s["sum"], g0 + k * 2 + h - 1)
                            t0 = (k * 2 + h) * G
                            ins = dve.tensor_tensor(oh[:, h, :, :], iota_row[:, None, :].to_broadcast([P, G, P]),
                                                    loc_d[:, bass.ds(t0, G)][:, :, None].to_broadcast([P, G, P]), ALU.is_equal)
                            if mode == "plain":
                                ins.then_inc(s["rhs"], 1)
                                return
                            if typed:
                                dve.tensor_tensor(oh8[:, h, :, :], iota8[:, None, :].to_broadcast([P, G, NTYPE]),
                                                  typ_d[:, bass.ds(t0, G)][:, :, None].to_broadcast([P, G, NTYPE]),
                                                  ALU.is_equal).then_inc(s["taken"], 1)
                                n_taken[h] = None
                                dve.wait_ge(s["taken"], tk0 + (k * 2 + h) + 1)
                                if mode == "types":
                                    dve.tensor_copy(rhs[:, h, :, NTYPE * f:width], oh8[:, h, :, :])
                            dve.wait_ge(s["got"][h], 16 * G * (k0 + k + 1))
                            if typed:
                                for j in range(G):
                                    ins = dve.tensor_tensor(
                                        rhs[:, h, j, 0:NTYPE * f].rearrange("p (r f) -> p r f", r=NTYPE),
                                        got[:, h, j, None, :].to_broadcast([P, NTYPE, f]),
                                        oh8[:, h, j, :, None].to_broadcast([P, NTYPE, f]), ALU.mult)
                                ins.then_inc(s["rhs"], 1)
                                return
                            dve.tensor_copy(rhs[:, h, :, 16:32], got[:, h, :, 0:16])
                            dve.tensor_tensor(gate[:, h, :], got[:, h, :, 16], hea_d[:, bass.ds(t0, G)], ALU.add).then_inc(s["taken"], 1)
                            dve.wait_ge(s["taken"], tk0 + (k * 2 + h) + 1)
                            dve.tensor_tensor(rhs[:, h, :, 0:16], got[:, h, :, 0:16],
                                              gate[:, h, :, None].to_broadcast([P, G, 16]), ALU.mult).then_inc(s["rhs"], 1)

                        def add(k, h, first):
                            dve.wait_ge(s["sum"], g0 + k * 2 + h + 1)
                            if not first:
                                dve.wait_ge(s["acc"], g0 + k * 2 + h)
                                if not (isinstance(k, int) and k == 0):
                                    dve.wait_ge(s["stored"][h], 16 * (k0 + k))
                                dve.scalar_tensor_tensor(acc[:, h, :], acc[:, 1 - h, :], keep_d[:, bass.ds(k * 2 + h, 1)],
                                                         banks[h][:, 0:width], ALU.mult, ALU.add).then_inc(s["acc"], 1)
                            else:
                                dve.tensor_copy(acc[:, h, :], banks[h][:, 0:width]).then_inc(s["acc"], 1)

                        n_taken = [0, 0]
                        tk0 = taken_n[0]
                        if mode != "plain":
                            taken_n[0] += NG
                        indices(0, 0, True)
                        indices(0, 1, True)
                        build(0, 0, True)
                        build(0, 1, True)
                        add(0, 0, True)

                        def turn_(k):
                            indices(k, 0, False)
                            build(k, 0, False)
                            add(k - 1, 1, False)
                            indices(k, 1, False)
                            build(k, 1, False)
                            add(k, 0, False)

                        turn_(1)
                        with dve.Fori(2, NG // 2) as k:
                            turn_(k)
                        add(NG // 2 - 1, 1, False)

        taken_n = [0]

        def turn_block(src, f, dst, extra=None):
            b_tr, b_cp = from_pe.base(len(CH)), to_pe.base(len(CH))
            with nc.Block() as block:
                @block.tensor
                def _(pe):
                    for c, (at, n) in enumerate(CH):
                        if c >= 2:
                            pe.wait_ge(to_pe.sem, b_cp + c - 1)
                        for j in range(n // P):
                            m = pe.transpose(banks[c % 2][0:f, j * P:(j + 1) * P], src[:, at // P + j, :], ident[:, :])
                        m.then_inc(from_pe.sem, 1)

                @block.vector
                def _(dve):
                    for c, (at, n) in enumerate(CH):
                        dve.wait_ge(from_pe.sem, b_tr + c + 1)
                        dve.tensor_copy(dst[0:f, at:at + n], banks[c % 2][0:f, 0:n]).then_inc(to_pe.sem, 1)

        def features(ws_, ins_, dst, m_, func, bias, add_to=None, mask=None):
            b_mm, b_ev = from_pe.base(len(CH)), from_act.base(len(CH))
            with nc.Block() as block:
                @block.tensor
                def _(pe):
                    for c, (at, n) in enumerate(CH):
                        if c >= 2:
                            pe.wait_ge(from_act.sem, b_ev + c - 1)
                        for q, (w_, i_) in enumerate(zip(ws_, ins_)):
                            m = pe.matmul(banks[c % 2][0:m_, 0:n], w_, i_[:, at:at + n], start=(q == 0), stop=(q == len(ws_) - 1))
                        m.then_inc(from_pe.sem, 1)

                @block.scalar
                def _(act):
                    for c, (at, n) in enumerate(CH):
                        act.wait_ge(from_pe.sem, b_mm + c + 1)
                        act.activation(dst[0:m_, at:at + n], banks[c % 2][0:m_, 0:n], func, bias=bias).then_inc(from_act.sem, 1)

                @block.vector
                def _(dve):
                    for c, (at, n) in enumerate(CH):
                        if add_to is None:
                            break
                        dve.wait_ge(from_act.sem, b_ev + c + 1)
                        v_chain(dve, dve.tensor_tensor(dst[:, at:at + n], dst[:, at:at + n], add_to[:, at:at + n], ALU.add))
                        dve.tensor_tensor(add_to[:, at:at + n], dst[:, at:at + n], mask[:, at:at + n], ALU.mult)

        def nodes(pairs, m_, bank):
            with nc.Block() as block:
                @block.tensor
                def _(pe):
                    for b in range(NB):
                        for q, (i_, w_) in enumerate(pairs):
                            pe.matmul(banks[bank][:, b * m_:(b + 1) * m_], i_[:, b * P:(b + 1) * P], w_,
                                      start=(q == 0), stop=(q == len(pairs) - 1))

        def row(t, f=FIN):
            return t[:, None, :].to_broadcast([P, NB, f])

        def each(t, f=FIN):
            return t[:, :, None].to_broadcast([P, NB, f])

        def layernorm(dve, b_act):
            mean, var, r = stat[:, 0, :], stat[:, 1, :], stat[:, 2, :]
            v_chain(dve, dve.tensor_reduce(mean, x[:, :, :], AX.X, ALU.add))
            v_chain(dve, dve.tensor_scalar(mean, mean, 1.0 / FIN, None, ALU.mult))
            v_chain(dve, dve.tensor_tensor(x[:, :, :], x[:, :, :], each(mean), ALU.subtract))
            v_chain(dve, dve.tensor_tensor(tmp[:, :, :], x[:, :, :], x[:, :, :], ALU.mult))
            v_chain(dve, dve.tensor_reduce(var, tmp[:, :, :], AX.X, ALU.add))
            dve.tensor_scalar(var, var, 1.0 / FIN, EPS, ALU.mult, ALU.add).then_inc(to_act.sem, 1)
            dve.wait_ge(from_act.sem, b_act + 1)
            v_chain(dve, dve.reciprocal(r, r))
            v_chain(dve, dve.tensor_tensor(x[:, :, :], x[:, :, :], each(r), ALU.mult))

        def root_step(act, b_to):
            act.wait_ge(to_act.sem, b_to + 1)
            act.activation(stat[:, 2, :], stat[:, 1, :], ACT.Sqrt).then_inc(from_act.sem, 1)

        def load(pairs):
            with nc.Block() as block:
                @block.sync
                def _(sp):
                    with nc.allow_non_contiguous_dma(reason="small weights"):
                        for d, s_ in pairs:
                            sp.dma_start(d, s_).then_inc(sp_dma.sem, 16)
                            sp_dma.n += 16
                    sp.wait_ge(sp_dma.sem, sp_dma.n)

        def save(pairs):
            load(pairs)

        def column(v):
            return v.rearrange("(p a) -> p a", a=1)

        def spread(v, n):
            return v.rearrange("(a n) -> a n", a=1).to_broadcast([P, n])

        with ExitStack() as st:
            w1a, w1b = sb("w1a", [16, 16], F32, st), sb("w1b", [16, 16], F32, st)
            w2a, w2b = sb("w2a", [16, 16], F32, st), sb("w2b", [16, 16], F32, st)
            b1a, b2a = sb("b1a", [16, 1], F32, st), sb("b2a", [16, 1], F32, st)
            b1b, b2b = sb("b1b", [P, 16], F32, st), sb("b2b", [P, 16], F32, st)
            eps = sb("eps", [P, 2], F32, st)
            h = sb("h", [P, NB, FIN], F32, st)
            agg = sb("agg0", [P, NB, FIN], F32, st)
            hT = sb("hT", [FIN, NP], F32, st)
            h1T = sb("h1T", [FIN, NP], F32, st)
            load([(w1a[:, :], a["L0_gnn_w1a"]), (w1b[:, :], a["L0_gnn_w1b"]), (w2a[:, :], a["L0_gnn_w2a"]),
                  (w2b[:, :], a["L0_gnn_w2b"]), (b1a[:, :], column(a["L0_gnn_b1a"])), (b2a[:, :], column(a["L0_gnn_b2a"])),
                  (b1b[:, :], spread(a["L0_gnn_b1b"], 16)), (b2b[:, :], spread(a["L0_gnn_b2b"], 16)),
                  (eps[:, 0:1], a["L0_gnn_eps1"].to_broadcast([P, 1])), (eps[:, 1:2], a["L0_gnn_eps2"].to_broadcast([P, 1]))])
            for layer, (wa_, ba_, wb_, bb_) in enumerate(((w1a, b1a, w1b, b1b), (w2a, b2a, w2b, b2b))):
                h_in = x if layer == 0 else h
                dst_pass("plain", x_tab if layer == 0 else h_tab, src_d, FIN, agg)
                with nc.Block() as block:
                    @block.vector
                    def _(dve):
                        if layer == 0:
                            v_chain(dve, dve.tensor_scalar(eps[:, :], eps[:, :], 1.0, None, ALU.add))
                        v_chain(dve, dve.scalar_tensor_tensor(agg[:, :, :], h_in[:, :, :], eps[:, layer:layer + 1],
                                                              agg[:, :, :], ALU.mult, ALU.add))
                turn_block(agg, FIN, hT)
                features([wa_[:, :]], [hT], h1T, FIN, ACT.Relu, ba_[:, 0:1])
                nodes([(h1T, wb_[:, :])], FIN, 0)
                out0 = banks[0][:, 0:NB * FIN].rearrange("p (b f) -> p b f", b=NB)
                if layer == 0:
                    with nc.Block() as block:
                        @block.vector
                        def _(dve):
                            v_chain(dve, dve.tensor_tensor(h[:, :, :], out0, row(bb_), ALU.add))
                            v_chain(dve, dve.tensor_scalar(h[:, :, :], h[:, :, :], 0.0, None, ALU.max))
                    save([(h_tab.rearrange("(b p) f -> p b f", p=P), h[:, :, :])])
                    continue
                b_to, b_fr = to_act.base(3), from_act.base(3)
                with nc.Block() as block:
                    @block.vector
                    def _(dve):
                        mx, sm = stat[:, 0, :], stat[:, 1, :]
                        v_chain(dve, dve.tensor_tensor(h[:, :, :], out0, row(bb_), ALU.add))
                        v_chain(dve, dve.tensor_reduce(mx, h[:, :, :], AX.X, ALU.max))
                        dve.tensor_tensor(h[:, :, :], h[:, :, :], each(mx), ALU.subtract).then_inc(to_act.sem, 1)
                        dve.wait_ge(from_act.sem, b_fr + 1)
                        dve.tensor_reduce(sm, tmp[:, :, :], AX.X, ALU.add).then_inc(to_act.sem, 1)
                        dve.wait_ge(from_act.sem, b_fr + 2)
                        v_chain(dve, dve.tensor_tensor(h[:, :, :], h[:, :, :], each(stat[:, 2, :]), ALU.subtract))
                        v_chain(dve, dve.tensor_tensor(x[:, :, :], x[:, :, :], h[:, :, :], ALU.add))
                        layernorm(dve, b_fr + 2)

                    @block.scalar
                    def _(act):
                        act.wait_ge(to_act.sem, b_to + 1)
                        act.activation(tmp[:, :, :], h[:, :, :], ACT.Exp).then_inc(from_act.sem, 1)
                        act.wait_ge(to_act.sem, b_to + 2)
                        act.activation(stat[:, 2, :], stat[:, 1, :], ACT.Ln).then_inc(from_act.sem, 1)
                        root_step(act, b_to + 2)

        m_sems = {n: sem("m_" + n) for n in ("idx", "oht", "ohm", "z1", "h1", "z2", "z2b", "h2", "sum", "acc")}
        m_got, m_ld = [sem("m_got0"), sem("m_got1")], [sem("m_ld0"), sem("m_ld1")]
        m_st = [sem("m_stored0"), sem("m_stored1")]

        def edge_mlp(layer, we, w2, b1, b2, agg):
            s, g0, k0 = m_sems, layer * NG, layer * (NG // 2)
            with ExitStack() as st:
                qidx = sb(f"qidx{layer}", [P, 2, G], I32, st)
                pidx = sb(f"pidx{layer}", [P, 2, 1], I32, st)
                qg = sb(f"qg{layer}", [P, 2, G, HID], F32, st)
                pb = sb(f"pb{layer}", [P, 2, HID], F32, st)
                places = sb(f"places{layer}", [P, 2, GE], F32, st)
                eat = sb(f"eat{layer}", [4, 2, GE], F32, st)
                oht = sb(f"oht{layer}", [P, 2, GE], F32, st)
                ohm = sb(f"ohm{layer}", [P, 2, G, P], F32, st)
                h1 = sb(f"h1{layer}", [P, 2, GE], F32, st)
                z2b = sb(f"z2b{layer}", [P, 2, G, HID], F32, st)
                h2 = sb(f"h2{layer}", [P, 2, G, HID], F32, st)
                acc = sb(f"macc{layer}", [P, 2, HID], F32, st)

                def late(n, h):
                    return layer > 0 or not isinstance(n, int) or n > 0

                with nc.Block() as block:
                    @block.gpsimd
                    def _(pool):
                        t0 = gates[0]
                        gates[0] += NG

                        def gather(k, h):
                            gate_before(pool, t0 + k * 2 + h)
                            pool.wait_ge(s["idx"], g0 + k * 2 + h + 1)
                            if late(k, h):
                                pool.wait_ge(s["z1"], g0 + k * 2 + h - 1)
                            pool_gate(pool)
                            pool.indirect_dma_start(pb[:, h, :], None, p_tab,
                                                    IndirectOffsetOnAxis(ap=pidx[:, h, 0:1], axis=0)).then_inc(m_got[h], 16)
                            for j in range(G):
                                pool.indirect_dma_start(qg[:, h, j, :], None, q_tab,
                                                        IndirectOffsetOnAxis(ap=qidx[:, h, j:j + 1], axis=0)).then_inc(m_got[h], 16)
                        gather(0, 0)
                        gather(0, 1)
                        with pool.Fori(1, NG // 2) as k:
                            gather(k, 0)
                            gather(k, 1)
                        for h in range(2):
                            pool.wait_ge(m_got[h], 16 * (G + 1) * (k0 + NG // 2))
                            pool.wait_ge(m_st[h], 16 * (k0 + NG // 2))
                        for b in range(NB):
                            pool.indirect_dma_start(agg[:, b, :], None, agg_s,
                                                    IndirectOffsetOnAxis(ap=last_s[:, b:b + 1], axis=0)).then_inc(pool_dma.sem, 16)
                        pool_dma.n += 16 * NB
                        pool.wait_ge(pool_dma.sem, pool_dma.n)

                    @block.sync
                    def _(sp):
                        def fetch(k, h):
                            if late(k, h):
                                sp.wait_ge(s["z1"], g0 + k * 2 + h - 1)
                                sp.wait_ge(s["oht"], g0 + k * 2 + h - 1)
                            at = (k * 2 + h) * GE
                            sp.dma_start(places[:, h, :], rows_s[0:1, bass.ds(at, GE)].to_broadcast([P, GE])).then_inc(m_ld[h], 16)
                            sp.dma_start(eat[:, h, :], rows_s[1:5, bass.ds(at, GE)]).then_inc(m_ld[h], 16)

                        def store(k, h):
                            sp.wait_ge(s["acc"], g0 + k * 2 + h + 1)
                            sp.dma_start(agg_s[bass.ds((k * 2 + h) * P, P), :], acc[:, h, :]).then_inc(m_st[h], 16)
                        fetch(0, 0)
                        fetch(0, 1)
                        fetch(1, 0)
                        fetch(1, 1)
                        with sp.Fori(2, NG // 2) as k:
                            store(k - 2, 0)
                            fetch(k, 0)
                            store(k - 2, 1)
                            fetch(k, 1)
                        for k in range(NG // 2 - 2, NG // 2):
                            store(k, 0)
                            store(k, 1)

                    @block.tensor
                    def _(pe):
                        def first_half(k, h):
                            pe.wait_ge(s["oht"], g0 + k * 2 + h + 1)
                            pe.wait_ge(m_ld[h], 32 * (k0 + k + 1))
                            pe.wait_ge(m_got[h], 16 * (G + 1) * (k0 + k + 1))
                            if late(k, h):
                                pe.wait_ge(s["h1"], g0 + k * 2 + h - 1)
                            z1 = banks[h]
                            pe.matmul(z1[:, :], pb[:, h, :], oht[:, h, :], start=True, stop=False)
                            pe.matmul(z1[:, :], we, eat[:, h, :], start=False, stop=False)
                            for j in range(G):
                                m = pe.matmul(z1[:, j * P:(j + 1) * P], qg[:, h, j, :], ident[:, :], start=False, stop=(j == G - 1))
                            m.then_inc(s["z1"], 1)

                        def second_half(k, h):
                            pe.wait_ge(s["h1"], g0 + k * 2 + h + 1)
                            if late(k, h):
                                pe.wait_ge(s["z2b"], g0 + k * 2 + h - 1)
                            for j in range(G):
                                m = pe.matmul(banks[2 + h][:, j * P:(j + 1) * P], h1[:, h, j * P:(j + 1) * P], w2, start=True, stop=True)
                            m.then_inc(s["z2"], 1)

                        def sums(k, h):
                            pe.wait_ge(s["h2"], g0 + k * 2 + h + 1)
                            pe.wait_ge(s["ohm"], g0 + k * 2 + h + 1)
                            if late(k, h):
                                pe.wait_ge(s["acc"], g0 + k * 2 + h - 1)
                            for j in range(G):
                                m = pe.matmul(banks[4 + h][:, 0:HID], ohm[:, h, j, :], h2[:, h, j, :], start=(j == 0), stop=(j == G - 1))
                            m.then_inc(s["sum"], 1)
                        K = NG // 2
                        first_half(0, 0)
                        first_half(0, 1)
                        second_half(0, 0)

                        def turn(k):
                            first_half(k, 0)
                            second_half(k - 1, 1)
                            sums(k - 1, 0)
                            first_half(k, 1)
                            second_half(k, 0)
                            sums(k - 1, 1)

                        turn(1)
                        with pe.Fori(2, K) as k:
                            turn(k)
                        second_half(K - 1, 1)
                        sums(K - 1, 0)
                        sums(K - 1, 1)

                    @block.scalar
                    def _(act):
                        def one(k, h):
                            act.wait_ge(s["z1"], g0 + k * 2 + h + 1)
                            if late(k, h):
                                act.wait_ge(s["z2"], g0 + k * 2 + h - 1)
                            act.activation(h1[:, h, :], banks[h][:, :], ACT.Silu, bias=b1).then_inc(s["h1"], 1)

                        def two(k, h):
                            act.wait_ge(s["z2b"], g0 + k * 2 + h + 1)
                            if late(k, h):
                                act.wait_ge(s["sum"], g0 + k * 2 + h - 1)
                            act.activation(h2[:, h, :, :], z2b[:, h, :, :], ACT.Silu).then_inc(s["h2"], 1)
                        K = NG // 2
                        one(0, 0)
                        one(0, 1)
                        two(0, 0)

                        def turn(k):
                            one(k, 0)
                            two(k - 1, 1)
                            one(k, 1)
                            two(k, 0)

                        turn(1)
                        with act.Fori(2, K) as k:
                            turn(k)
                        two(K - 1, 1)

                    @block.vector
                    def _(dve):
                        def indices(k, h):
                            if late(k, h):
                                dve.wait_ge(m_got[h], 16 * (G + 1) * (k0 + k))
                            dve.tensor_copy(pidx[:, h, :], blk_s[:, bass.ds(k * 2 + h, 1)])
                            dve.tensor_copy(qidx[:, h, :], col_s[:, bass.ds((k * 2 + h) * G, G)]).then_inc(s["idx"], 1)

                        def build(k, h):
                            if late(k, h):
                                dve.wait_ge(s["z1"], g0 + k * 2 + h - 1)
                            dve.wait_ge(m_ld[h], 32 * (k0 + k + 1))
                            dve.tensor_scalar(oht[:, h, :], places[:, h, :], iota_p[:, 0:1], None, ALU.is_equal).then_inc(s["oht"], 1)

                        def build_m(k, h):
                            if late(k, h):
                                dve.wait_ge(s["sum"], g0 + k * 2 + h - 1)
                            for j in range(G):
                                t = (k * 2 + h) * G + j
                                m = dve.tensor_scalar(ohm[:, h, j, :], iota_row[:, :], loc_s[:, bass.ds(t, 1)],
                                                      w_s[:, bass.ds(t, 1)], ALU.is_equal, ALU.mult)
                            m.then_inc(s["ohm"], 1)

                        def bias(k, h):
                            dve.wait_ge(s["z2"], g0 + k * 2 + h + 1)
                            if late(k, h):
                                dve.wait_ge(s["h2"], g0 + k * 2 + h - 1)
                            dve.tensor_tensor(z2b[:, h, :, :], banks[2 + h][:, :].rearrange("p (j f) -> p j f", j=G),
                                              b2[:, None, :].to_broadcast([P, G, HID]), ALU.add).then_inc(s["z2b"], 1)

                        def add(k, h):
                            dve.wait_ge(s["sum"], g0 + k * 2 + h + 1)
                            if late(k, h):
                                dve.wait_ge(m_st[h], 16 * (k0 + k))
                            if isinstance(k, int) and k == 0 and h == 0:
                                dve.tensor_copy(acc[:, h, :], banks[4 + h][:, 0:HID]).then_inc(s["acc"], 1)
                                return
                            dve.wait_ge(s["acc"], g0 + k * 2 + h)
                            dve.scalar_tensor_tensor(acc[:, h, :], acc[:, 1 - h, :], keep_s[:, bass.ds(k * 2 + h, 1)],
                                                     banks[4 + h][:, 0:HID], ALU.mult, ALU.add).then_inc(s["acc"], 1)
                        K = NG // 2
                        indices(0, 0)
                        indices(0, 1)
                        build(0, 0)
                        build(0, 1)
                        build_m(0, 0)
                        bias(0, 0)

                        def turn(k):
                            indices(k, 0)
                            build(k, 0)
                            build_m(k - 1, 1)
                            bias(k - 1, 1)
                            add(k - 1, 0)
                            indices(k, 1)
                            build(k, 1)
                            build_m(k, 0)
                            bias(k, 0)
                            add(k - 1, 1)

                        turn(1)
                        with dve.Fori(2, K) as k:
                            turn(k)
                        build_m(K - 1, 1)
                        bias(K - 1, 1)
                        add(K - 1, 0)
                        add(K - 1, 1)

        with ExitStack() as st:
            hT = sb("hidT", [P, NP], F32, st)
            aggT = sb("aggT", [P, NP], F32, st)
            nT = sb("nT", [P, NP], F32, st)
            maskT = sb("maskT", [P, NP], F32, st)
            agg = sb("agg1", [P, NB, HID], F32, st)
            wpq = sb("wpq", [P, 2, HID], F32, st)
            pq = sb("pq", [P, 2, 2, HID], F32, st)
            we = sb("we", [4, HID], F32, st)
            w2 = sb("w2", [P, HID], F32, st)
            b1, b2 = sb("b1", [P, 1], F32, st), sb("b2", [P, HID], F32, st)
            wn1 = sb("wn1", [P, 2, HID], F32, st)
            wn2 = sb("wn2", [P, HID], F32, st)
            bn1, bn2 = sb("bn1", [P, 1], F32, st), sb("bn2", [P, 1], F32, st)
            wemb, bemb = sb("wemb", [FIN, HID], F32, st), sb("bemb", [P, 1], F32, st)
            wout, bout = sb("wout", [P, FIN], F32, st), sb("bout", [P, FIN], F32, st)
            pq_out = [sem("pq_out0"), sem("pq_out1")]
            pq_n = [0, 0]

            with nc.Block() as block:
                @block.vector
                def _(dve):
                    v_chain(dve, dve.memset(maskT[:, :], 0.0))
            load([(maskT[:, 0:N], a["node_vec1"].rearrange("n a -> a n").to_broadcast([P, N])),
                  (wemb[:, :], a["L1_gnn_emb_w"]), (bemb[:, :], column(a["L1_gnn_emb_b"])),
                  (wout[:, :], a["L1_gnn_out_w"]), (bout[:, :], spread(a["L1_gnn_out_b"], FIN))])
            turn_block(x, FIN, xT)
            features([wemb[:, :]], [xT], hT, HID, ACT.Identity, bemb[:, 0:1])
            for layer in range(L):
                ew1 = a["L1_gnn_edge_w1"][layer]
                nw1 = a["L1_gnn_node_w1"][layer]
                load([(wpq[:, 0, :], ew1[0:HID, :]), (wpq[:, 1, :], ew1[HID:2 * HID, :]), (we[:, :], ew1[2 * HID:2 * HID + 4, :]),
                      (b1[:, :], column(a["L1_gnn_edge_b1"][layer])), (w2[:, :], a["L1_gnn_edge_w2"][layer]),
                      (b2[:, :], spread(a["L1_gnn_edge_b2"][layer], HID)),
                      (wn1[:, 0, :], nw1[0:HID, :]), (wn1[:, 1, :], nw1[HID:2 * HID, :]),
                      (bn1[:, :], column(a["L1_gnn_node_b1"][layer])), (wn2[:, :], a["L1_gnn_node_w2"][layer]),
                      (bn2[:, :], column(a["L1_gnn_node_b2"][layer]))])
                b_mm, b_cp = from_pe.base(NB), to_pe.base(NB)
                with nc.Block() as block:
                    @block.tensor
                    def _(pe):
                        for b in range(NB):
                            if b >= 2:
                                pe.wait_ge(to_pe.sem, b_cp + b - 1)
                            pe.matmul(banks[b % 2][:, 0:2 * HID], hT[:, b * P:(b + 1) * P],
                                      wpq[:, :, :].rearrange("p k f -> p (k f)"), start=True, stop=True).then_inc(from_pe.sem, 1)

                    @block.vector
                    def _(dve):
                        for b in range(NB):
                            dve.wait_ge(from_pe.sem, b_mm + b + 1)
                            if pq_n[b % 2] > 0:
                                dve.wait_ge(pq_out[b % 2], pq_n[b % 2])
                            dve.tensor_copy(pq[:, b % 2, :, :], banks[b % 2][:, 0:2 * HID].rearrange("p (k f) -> p k f", k=2)).then_inc(to_pe.sem, 1)
                            pq_n[b % 2] += 32
                    @block.sync
                    def _(sp):
                        for b in range(NB):
                            sp.wait_ge(to_pe.sem, b_cp + b + 1)
                            sp.dma_start(p_tab[b * P:(b + 1) * P, :], pq[:, b % 2, 0, :]).then_inc(pq_out[b % 2], 16)
                            sp.dma_start(q_tab[b * P:(b + 1) * P, :], pq[:, b % 2, 1, :]).then_inc(pq_out[b % 2], 16)
                        for h in range(2):
                            sp.wait_ge(pq_out[h], pq_n[h])
                edge_mlp(layer, we[:, :], w2[:, :], b1[:, 0:1], b2, agg)
                turn_block(agg, HID, aggT)
                features([wn1[:, 0, :], wn1[:, 1, :]], [hT, aggT], nT, HID, ACT.Silu, bn1[:, 0:1])
                features([wn2[:, :]], [nT], aggT, HID, ACT.Identity, bn2[:, 0:1], add_to=hT, mask=maskT)
            nodes([(hT, wout[:, :])], FIN, 0)
            b_to, b_fr = to_act.base(1), from_act.base(1)
            with nc.Block() as block:
                @block.vector
                def _(dve):
                    o = banks[0][:, 0:NB * FIN].rearrange("p (b f) -> p b f", b=NB)
                    v_chain(dve, dve.tensor_tensor(tmp[:, :, :], o, row(bout), ALU.add))
                    v_chain(dve, dve.tensor_tensor(tmp[:, :, :], tmp[:, :, :], each(nodev), ALU.mult))
                    v_chain(dve, dve.tensor_tensor(x[:, :, :], x[:, :, :], tmp[:, :, :], ALU.add))
                    layernorm(dve, b_fr)

                @block.scalar
                def _(act):
                    root_step(act, b_to)

        with ExitStack() as st:
            wcT = sb("wcT", [NBAS, NREL], F32, st)
            vv = sb("vv", [NBAS, 16, 16], F32, st)
            gg = sb("gg", [NREL, 16, 16], F32, st)
            wr = sb("wr", [FIN, NREL, 17], F32, st)
            yb = sb("yb", [P, 2, NREL * 17], F32, st)
            wl = sb("wl", [FIN, NREL, 16], F32, st)
            agg = sb("agg2", [P, NB, 32], F32, st)
            s3 = sb("s3", [P, NB], F32, st)
            y_out = [sem("y_out0"), sem("y_out1")]
            load([(wcT[:, :], a["L2_gnn_w_comp"].rearrange("r b -> b r")),
                  (vv[:, :, :], a["L2_gnn_weight"].rearrange("b i o -> (b i o)").rearrange("(i b o) -> b i o", i=16, b=NBAS))])
            with nc.Block() as block:
                @block.tensor
                def _(pe):
                    pe.matmul(banks[0][0:NREL, 0:256], wcT[:, :], vv[:, :, :].rearrange("b i o -> b (i o)"), start=True, stop=True)
            with nc.Block() as block:
                @block.vector
                def _(dve):
                    v_chain(dve, dve.tensor_copy(gg[:, :, :], banks[0][0:NREL, 0:256].rearrange("r (i o) -> r i o", i=16)))
            save([(g_tab.rearrange("(i r o) -> r i o", i=16, r=NREL), gg[:, :, :])])
            load([(wl[:, :, :], g_tab.rearrange("(r i o) -> i r o", r=NREL, i=16))])
            turn_block(x, FIN, xT)
            b_mm, b_cp = from_pe.base(NB * 3), to_pe.base(NB * 3)
            with nc.Block() as block:
                @block.vector
                def _(dve):
                    v_chain(dve, dve.tensor_copy(wr[:, :, 0:16], wl[:, :, :]))
                    v_chain(dve, dve.tensor_copy(wr[:, :, 16:17], a_cols[:, None, 0:1].to_broadcast([FIN, NREL, 1])))
                    v_chain(dve, dve.tensor_tensor(tmp[:, :, :], x[:, :, :], a_rows[:, 1:2, :].to_broadcast([P, NB, FIN]), ALU.mult))
                    v_chain(dve, dve.tensor_reduce(s3[:, :], tmp[:, :, :], AX.X, ALU.add))
            YC = NREL * 17 // 3
            with nc.Block() as block:
                @block.tensor
                def _(pe):
                    for b in range(NB):
                        for c in range(3):
                            n = 3 * b + c
                            if n >= 6:
                                pe.wait_ge(to_pe.sem, b_cp + n - 5)
                            pe.matmul(banks[n % 6][:, 0:YC], xT[:, b * P:(b + 1) * P],
                                      wr[:, :, :].rearrange("i r o -> i (r o)")[:, c * YC:(c + 1) * YC], start=True, stop=True).then_inc(from_pe.sem, 1)

                @block.vector
                def _(dve):
                    for b in range(NB):
                        if b >= 2:
                            dve.wait_ge(y_out[b % 2], 16 * (b // 2))
                        for c in range(3):
                            n = 3 * b + c
                            dve.wait_ge(from_pe.sem, b_mm + n + 1)
                            dve.tensor_copy(yb[:, b % 2, c * YC:(c + 1) * YC], banks[n % 6][:, 0:YC]).then_inc(to_pe.sem, 1)

                @block.sync
                def _(sp):
                    for b in range(NB):
                        sp.wait_ge(to_pe.sem, b_cp + 3 * b + 3)
                        sp.dma_start(y_tab[b * P * NREL:(b + 1) * P * NREL, :].rearrange("(p r) o -> p (r o)", p=P),
                                     yb[:, b % 2, :]).then_inc(y_out[b % 2], 16)
                    sp.wait_ge(y_out[0], 16 * ((NB + 1) // 2))
                    sp.wait_ge(y_out[1], 16 * (NB // 2))
            dst_pass("msg", y_tab, rel_d, 17, agg)
            b_to, b_fr = to_act.base(1), from_act.base(1)
            with nc.Block() as block:
                @block.vector
                def _(dve):
                    v_chain(dve, dve.tensor_tensor(tmp[:, :, :], agg[:, :, 16:32], each(s3), ALU.mult))
                    v_chain(dve, dve.tensor_tensor(tmp[:, :, :], tmp[:, :, :], agg[:, :, 0:16], ALU.add))
                    v_chain(dve, dve.tensor_tensor(x[:, :, :], x[:, :, :], tmp[:, :, :], ALU.add))
                    layernorm(dve, b_fr)

                @block.scalar
                def _(act):
                    root_step(act, b_to)

        with ExitStack() as st:
            w1 = sb("rw1", [P, 32], F32, st)
            r1 = sb("rr1", [FIN, 32], F32, st)
            bb1 = sb("rb1", [32, 1], F32, st)
            w2_ = sb("rw2", [P, 2, 16], F32, st)
            r2 = sb("rr2", [32, 16], F32, st)
            bb2 = sb("rb2", [P, 16], F32, st)
            mT = sb("mT", [P, 2, NP], F32, st)
            h3T = sb("h3T", [32, NP], F32, st)
            h3 = sb("h3", [P, NB, 32], F32, st)
            mean = sb("mean", [P, NB, 256], F32, st)
            load([(w1[:, :], a["L3_gnn_W1"].rearrange("r i o -> (r i) o")), (r1[:, :], a["L3_gnn_root1"]),
                  (bb1[:, :], column(a["L3_gnn_b1"])),
                  (w2_[:, :, :], a["L3_gnn_W2"].rearrange("r i o -> (r i) o").rearrange("(c k) o -> k c o", c=2)),
                  (r2[:, :], a["L3_gnn_root2"]), (bb2[:, :], spread(a["L3_gnn_b2"], 16)),
                  (x_tab.rearrange("(b p) f -> p b f", p=P), x[:, :, :])])
            with ExitStack() as st2:
                agg = sb("agg3", [P, NB, 136], F32, st2)
                dst_pass("types", x_tab, src_d, 16, agg)
                with nc.Block() as block:
                    @block.vector
                    def _(dve):
                        v_chain(dve, dve.tensor_scalar(nrm_d[:, :, :], agg[:, :, 128:136], 1.0, None, ALU.max))
                        v_chain(dve, dve.reciprocal(nrm_d[:, :, :], nrm_d[:, :, :]))
                        for b in range(NB):
                            dve.tensor_tensor(mean[:, b, 0:128].rearrange("p (r f) -> p r f", r=NTYPE),
                                              agg[:, b, 0:128].rearrange("p (r f) -> p r f", r=NTYPE),
                                              nrm_d[:, b, :, None].to_broadcast([P, NTYPE, 16]), ALU.mult)
            turn_block(mean[:, :, 0:128], P, mT[:, 0, :])
            turn_block(x, FIN, xT)
            features([w1[:, :], r1[:, :]], [mT[:, 0, :], xT], h3T, 32, ACT.Relu, bb1[:, 0:1])
            b_mm, b_cp = from_pe.base(2), to_pe.base(1)
            with nc.Block() as block:
                @block.tensor
                def _(pe):
                    for b in range(NB):
                        m = pe.transpose(banks[b // 16][:, (b % 16) * 32:(b % 16 + 1) * 32], h3T[:, b * P:(b + 1) * P], ident[0:32, 0:32])
                        if b in (15, NB - 1):
                            m.then_inc(from_pe.sem, 1)

                @block.vector
                def _(dve):
                    dve.wait_ge(from_pe.sem, b_mm + 1)
                    dve.tensor_copy(h3[:, 0:16, :], banks[0][:, :].rearrange("p (b f) -> p b f", f=32))
                    dve.wait_ge(from_pe.sem, b_mm + 2)
                    dve.tensor_copy(h3[:, 16:NB, :], banks[1][:, 0:(NB - 16) * 32].rearrange("p (b f) -> p b f", f=32)).then_inc(to_pe.sem, 1)
            save([(h3_tab.rearrange("(b p) f -> p b f", p=P), h3[:, :, :])])
            dst_pass("types_only", h3_tab, src_d, 32, mean)
            with nc.Block() as block:
                @block.vector
                def _(dve):
                    for b in range(NB):
                        v = mean[:, b, :].rearrange("p (r f) -> p r f", r=NTYPE)
                        dve.tensor_tensor(v, v, nrm_d[:, b, :, None].to_broadcast([P, NTYPE, 32]), ALU.mult)
            turn_block(mean[:, :, 0:128], P, mT[:, 0, :])
            turn_block(mean[:, :, 128:256], P, mT[:, 1, :])
            nodes([(mT[:, 0, :], w2_[:, 0, :]), (mT[:, 1, :], w2_[:, 1, :]), (h3T, r2[:, :])], FIN, 0)
            b_to, b_fr = to_act.base(1), from_act.base(1)
            with nc.Block() as block:
                @block.vector
                def _(dve):
                    o = banks[0][:, 0:NB * FIN].rearrange("p (b f) -> p b f", b=NB)
                    v_chain(dve, dve.tensor_tensor(tmp[:, :, :], o, row(bb2), ALU.add))
                    v_chain(dve, dve.tensor_tensor(x[:, :, :], x[:, :, :], tmp[:, :, :], ALU.add))
                    layernorm(dve, b_fr)

                @block.scalar
                def _(act):
                    root_step(act, b_to)
            full = (N // P) * P
            save([(out[0:full, :].rearrange("(b p) f -> p b f", p=P), x[:, 0:N // P, :]),
                  (out[full:N, :], x[0:N - full, NB - 1, :])])


def kernel(**inputs):
    import numpy as _np
    import concourse.bacc as _bacc
    from concourse import mybir as _mybir
    from concourse.bass_utils import run_bass_kernel_spmd as _run

    nc = _bacc.Bacc("TRN2", target_bir_lowering=False, num_devices=1)
    arrays, args = {}, {}
    for name, v in inputs.items():
        v = _np.ascontiguousarray(v)
        if v.ndim == 0:
            v = v.reshape(1, 1)
        arrays[f"in_{name}_dram"] = v
        args[name] = nc.dram_tensor(f"in_{name}_dram", v.shape, _mybir.dt.from_np(v.dtype), kind="ExternalInput").ap()
    out = nc.dram_tensor("out_0_dram", (N, FIN), F32, kind="ExternalOutput").ap()
    gnn_kernel(nc, args, out)
    r = _run(nc, [arrays], core_ids=[0])
    return r.results[0]["out_0_dram"]
```

```python
from contextlib import ExitStack

import concourse.bass as bass
from concourse import mybir
from concourse.bass import IndirectOffsetOnAxis

F32 = mybir.dt.float32
I32 = mybir.dt.int32
ALU = mybir.AluOpType
ACT = mybir.ActivationFunctionType
AX = mybir.AxisListType

P = 128
N, FIN = 3125, 16
E = 103125
NB = -(-N // P)
NP = NB * P
G = 4
GE = G * P
NG = E // GE + NB
U = 4
NG = -(-NG // U) * U
K = NG // U
NT = NG * G
T = -(-E // (P * 8)) * 8
FULL = E // T
TAIL = E - FULL * T
W = 8
HID, L = 128, 4
NREL, NBAS, NTYPE = 90, 30, 8
NOWHERE = 999.0
CH = [(c, min(512, NP - c)) for c in range(0, NP, 512)]
EPS = 1e-5


def gnn_kernel(nc, a, out):
    with ExitStack() as ctx:
        def sb(name, shape, dt=F32, st=None):
            return (st or ctx).enter_context(nc.sbuf_tensor(name, shape, dt))

        def dram(name, shape, dt=F32):
            return nc.dram_tensor(name, shape, dt, kind="Internal").ap()

        def sem(name):
            return ctx.enter_context(nc.semaphore(name))

        class Chain:
            def __init__(self, name):
                self.sem, self.n = sem(name), 0

            def __call__(self, eng, ins, by=1):
                self.n += by
                ins.then_inc(self.sem, by)
                eng.wait_ge(self.sem, self.n)

        class Signal:
            def __init__(self, name):
                self.sem, self.n = sem(name), 0

            def base(self, adds):
                at = self.n
                self.n += adds
                return at

        v_chain, a_chain, p_chain = Chain("v_chain"), Chain("a_chain"), Chain("p_chain")
        sp_dma, pool_dma, act_dma = Chain("sp_dma"), Chain("pool_dma"), Chain("act_dma")
        to_pe, from_pe = Signal("vector_to_pe"), Signal("pe_to_vector")
        to_act, from_act = Signal("vector_to_act"), Signal("act_to_vector")

        gate_passed = sem("gate_passed")

        def pool_gate(pool):
            pool.sem_inc(gate_passed, 1)

        list_s = dram("list_by_src", [P * NT + T, W])
        list_d = dram("list_by_dst", [P * NT + T, W])
        rows_s = dram("rows_by_src", [5, NT * P])
        agg_s = dram("agg_by_src", [NG * P, HID])
        agg_d = {w: dram(f"agg_by_dst_{w}", [NG * P, w]) for w in (16, 32, 136, 256)}
        p_tab = dram("p_tab", [NP, HID])
        q_tab = dram("q_tab", [NP, HID])
        x_tab = dram("x_tab", [NP, FIN])
        h_tab = dram("h_tab", [NP, FIN])
        h3_tab = dram("h3_tab", [NP, 32])
        g_tab = dram("g_tab", [FIN * NREL * 16])
        y_tab = dram("y_tab", [NP * NREL, 17])

        ident = sb("ident", [P, P])
        iota_row = sb("iota_row", [P, P])
        iota_p = sb("iota_p", [P, 1])
        iota8 = sb("iota8", [P, NTYPE])
        x = sb("x", [P, NB, FIN])
        nodev = sb("nodev", [P, NB])
        tmp = sb("tmp", [P, NB, FIN])
        tmp2 = sb("tmp2", [P, NB, FIN])
        stat = sb("stat", [P, 3, NB])
        epst = sb("epst", [P, 1])
        xT = sb("xT", [FIN, NP])
        col_s = sb("col_s", [P, NT], I32)
        loc_s = sb("loc_s", [P, NT])
        w_s = sb("w_s", [P, NT])
        blk_s = sb("blk_s", [P, NG], I32)
        keep_s = sb("keep_s", [P, NG])
        last_s = sb("last_s", [P, NB], I32)
        src_d = sb("src_d", [P, NT], I32)
        rel_d = sb("rel_d", [P, NT], I32)
        loc_d = sb("loc_d", [P, NT])
        typ_d = sb("typ_d", [P, NT])
        hea_d = sb("hea_d", [P, NT])
        keep_d = sb("keep_d", [P, NG])
        last_d = sb("last_d", [P, NB], I32)
        nrm_d = sb("nrm_d", [P, NB, NTYPE])
        a_rows = sb("a_rows", [P, 2, FIN])
        a_cols = sb("a_cols", [FIN, 3])
        zero_row = sb("zero_row", [P, HID])

        banks = [ctx.enter_context(nc.psum_tensor(f"bank{i}", [P, 512], F32)) for i in range(8)]

        def by_edge(dst, src, lo=0, hi=T):
            pairs, full16 = [], FULL // 16 * 16
            for p0, p1 in ((0, full16), (full16, FULL)):
                v = src[p0 * T:p1 * T]
                v = v.rearrange("(p t) -> p t", t=T) if len(src.shape) == 1 else v.rearrange("(p t) k -> p t k", t=T)
                pairs.append((dst[p0:p1], v[:, lo:hi]))
            n = min(hi, TAIL) - lo
            if n > 0:
                v = src[FULL * T + lo:FULL * T + lo + n]
                v = v.rearrange("(p t) -> p t", p=1) if len(src.shape) == 1 else v.rearrange("(p t) k -> p t k", p=1)
                pairs.append((dst[FULL:FULL + 1, 0:n], v))
            return pairs

        with ExitStack() as st:
            ws = sb("ws", [FIN, FIN], F32, st)
            wa = sb("wa", [FIN, 3], F32, st)
            wab = sb("wab", [FIN, 2, P], F32, st)
            ones16 = sb("ones16", [FIN, P], F32, st)
            b_pe, b_fpe = to_pe.base(1), from_pe.base(1)
            s_init = sem("s_init")
            with nc.Block() as block:
                @block.gpsimd
                def _(pool):
                    p_chain(pool, pool.memset(ident[:, :], 0.0))
                    p_chain(pool, pool.affine_select(out=ident[:, :], in_=ident[:, :], compare_op=ALU.not_equal,
                                                     fill=1.0, base=0, pattern=[[-1, P]], channel_multiplier=1))
                    kw = dict(allow_small_or_imprecise_dtypes=True)
                    p_chain(pool, pool.iota(iota_row[:, :], [[1, P]], base=0, channel_multiplier=0, **kw))
                    p_chain(pool, pool.iota(iota_p[:, :], [[0, 1]], base=0, channel_multiplier=1, **kw))
                    p_chain(pool, pool.iota(iota8[:, :], [[1, NTYPE]], base=0, channel_multiplier=0, **kw))

                @block.sync
                def _(sp):
                    sp.wait_ge(s_init, 1)
                    with nc.allow_non_contiguous_dma(reason="small weights"):
                        sp_dma(sp, sp.dma_start(ws[:, :], a["L2_gnn_Ws"]), 16)
                        sp_dma(sp, sp.dma_start(wa[:, :], a["L2_gnn_Wa"].rearrange("a (k o) -> o (a k)", k=3)), 16)
                        full = (N // P) * P
                        sp_dma(sp, sp.dma_start(x[:, 0:N // P, :], a["x"][0:full, :].rearrange("(b p) f -> p b f", p=P)), 16)
                        sp_dma(sp, sp.dma_start(x[0:N - full, NB - 1, :], a["x"][full:N, :]), 16)
                        nv = a["node_vec1"].rearrange("n a -> (n a)")
                        sp_dma(sp, sp.dma_start(nodev[:, 0:N // P], nv[0:full].rearrange("(b p) -> p b", p=P)), 16)
                        sp_dma(sp, sp.dma_start(nodev[0:N - full, NB - 1:NB], nv[full:N].rearrange("(p a) -> p a", a=1)), 16)
                        sp_dma(sp, sp.dma_start(x_tab.rearrange("(b p) f -> p b f", p=P), x[:, :, :]), 16)

                n_dma = sp_dma.n

                @block.vector
                def _(dve):
                    v_chain(dve, dve.memset(x[:, :, :], 0.0))
                    v_chain(dve, dve.memset(zero_row[:, :], 0.0))
                    v_chain(dve, dve.memset(epst[:, :], EPS))
                    v_chain(dve, dve.memset(ones16[:, :], 1.0))
                    dve.memset(nodev[:, :], 0.0).then_inc(s_init, 1)
                    dve.wait_ge(sp_dma.sem, n_dma)
                    v_chain(dve, dve.tensor_scalar(wab[:, 0, :], ones16[:, :], wa[:, 1:2], None, ALU.mult))
                    dve.tensor_scalar(wab[:, 1, :], ones16[:, :], wa[:, 2:3], None, ALU.mult).then_inc(to_pe.sem, 1)
                    dve.wait_ge(from_pe.sem, b_fpe + 1)
                    v_chain(dve, dve.tensor_copy(a_rows[:, :, :], banks[0][:, 0:32].rearrange("p (k i) -> p k i", k=2)))
                    v_chain(dve, dve.tensor_copy(a_cols[:, :], banks[1][0:FIN, 0:3]))

                @block.tensor
                def _(pe):
                    pe.wait_ge(to_pe.sem, b_pe + 1)
                    pe.matmul(banks[0][:, 0:16], wab[:, 0, :], ws[:, :], start=True, stop=True)
                    pe.matmul(banks[0][:, 16:32], wab[:, 1, :], ws[:, :], start=True, stop=True)
                    pe.matmul(banks[1][0:FIN, 0:3], ws[:, :], wa[:, :], start=True, stop=True).then_inc(from_pe.sem, 1)

        with ExitStack() as st:
            srct = sb("srct", [P, T], I32, st)
            dstt = sb("dstt", [P, T], I32, st)
            rec_s = sb("rec_s", [P, T, W], F32, st)
            rec_d = sb("rec_d", [P, T, W], F32, st)
            pos_i = [sb("pos_s", [P, T], I32, st), sb("pos_d", [P, T], I32, st)]
            tri = sb("tri", [P, P], F32, st)
            ones = sb("ones", [P, P], F32, st)
            cnt = sb("cnt", [P, NB], F32, st)
            first = sb("first", [P, NB], F32, st)
            nxt = sb("nxt", [P, NB], F32, st)
            tot = sb("tot", [P, NB], F32, st)
            toti = sb("toti", [P, NB], I32, st)
            delta = sb("delta", [P, NB], F32, st)
            iota_g = sb("iota_g", [P, NG], F32, st)
            accg = sb("accg", [P, NG], F32, st)
            s_load, s_pad, s_cnt, s_tri = sem("s_load"), sem("s_pad"), sem("s_cnt"), sem("s_tri")
            s_const, s_pos, s_ring, s_t8 = sem("s_const"), sem("s_pos"), sem("s_ring"), sem("s_t8")
            scattered = [sem("scattered0"), sem("scattered1")]
            with ExitStack() as st2:
                padt = sb("padt", [P, NT // 8, W], F32, st2)
                ew = sb("ew", [P, T], F32, st2)
                ea4 = sb("ea4", [P, T, 4], F32, st2)
                posf = sb("posf", [P, T], F32, st2)
                ea16 = sb("ea16", [P, T // 4, FIN], F32, st2)
                blkf = sb("blkf", [P, T], F32, st2)
                onehot = sb("onehot", [P, T], F32, st2)
                run = sb("run", [P, T], F32, st2)
                ti = onehot[:, :].bitcast(I32)
                t8 = run[:, :].bitcast(I32)
                s_ea = sem("s_ea")
                s_eafree = sem("s_eafree")
                with nc.Block() as block:
                    @block.gpsimd
                    def _(pool):
                        kw = dict(allow_small_or_imprecise_dtypes=True)
                        p_chain(pool, pool.memset(ones[:, :], 1.0))
                        p_chain(pool, pool.memset(tri[:, :], 1.0))
                        p_chain(pool, pool.affine_select(out=tri[:, :], in_=tri[:, :], compare_op=ALU.is_gt, fill=0.0,
                                                         base=0, pattern=[[1, P]], channel_multiplier=-1))
                        pool.iota(iota_g[:, :], [[1, NG]], base=0, channel_multiplier=0, **kw).then_inc(s_const, 1)

                    @block.sync
                    def _(sp):
                        sp.wait_ge(s_pad, 1)
                        with nc.allow_non_contiguous_dma(reason="records"):
                            for t, v in ((srct, a["src"]), (dstt, a["dst"]), (t8, a["edge_type_8"]), (ti, a["edge_type_90"]),
                                         (ew, a["edge_weight1"].rearrange("e a -> (e a)")), (ea4, a["edge_attr_4"])):
                                for d, v_ in by_edge(t, v):
                                    sp.dma_start(d, v_).then_inc(s_load, 16)
                            for lst in (list_s, list_d):
                                view = lst[0:P * NT, :].rearrange("(p t) w -> p t w", p=P)
                                for c in range(8):
                                    sp.dma_start(view[:, c * (NT // 8):(c + 1) * (NT // 8), :], padt[:, :, :]).then_inc(s_t8, 16)
                            for q in range(4):
                                if q:
                                    sp.wait_ge(s_eafree, q)
                                for d, v_ in by_edge(ea16, a["edge_attr_16"], q * (T // 4), (q + 1) * (T // 4)):
                                    sp.dma_start(d, v_).then_inc(s_ea, 16)
                            sp.wait_ge(s_t8, 256)

                    @block.tensor
                    def _(pe):
                        pe.wait_ge(s_const, 1)
                        for k in range(2):
                            pe.wait_ge(s_cnt, k + 1)
                            pe.matmul(banks[0][:, 0:NB], tri[:, :], cnt[:, :], start=True, stop=True)
                            pe.matmul(banks[1][:, 0:NB], ones[:, :], cnt[:, :], start=True, stop=True).then_inc(s_tri, 1)

                    @block.vector
                    def _(dve):
                        v_chain(dve, dve.memset(padt[:, :, :], 0.0))
                        v_chain(dve, dve.memset(padt[:, :, 0:1], NOWHERE))
                        v_chain(dve, dve.memset(rec_s[:, :, :], 0.0))
                        v_chain(dve, dve.memset(rec_d[:, :, :], 0.0))
                        v_chain(dve, dve.memset(ea16[:, :, :], 0.0))
                        v_chain(dve, dve.memset(ew[:, :], 0.0))
                        v_chain(dve, dve.memset(ea4[:, :, :], 0.0))
                        v_chain(dve, dve.memset(ti, 0))
                        v_chain(dve, dve.memset(t8, 0))
                        v_chain(dve, dve.memset(srct[:, :], 1 << 20))
                        dve.memset(dstt[:, :], 1 << 20).then_inc(s_pad, 1)
                        dve.wait_ge(s_load, 6 * 3 * 16)
                        v_chain(dve, dve.tensor_copy(rec_s[:, :, 2], ew[:, :]))
                        v_chain(dve, dve.tensor_copy(rec_s[:, :, 3:7], ea4[:, :, :]))
                        v_chain(dve, dve.tensor_copy(rec_d[:, :, 3], t8))
                        v_chain(dve, dve.tensor_copy(rec_d[:, :, 1].bitcast(I32), srct[:, :]))
                        v_chain(dve, dve.scalar_tensor_tensor(rec_d[:, :, 2].bitcast(I32), srct[:, :], float(NREL), ti, ALU.mult, ALU.add))
                        v_chain(dve, dve.tensor_copy(rec_s[:, :, 1].bitcast(I32), dstt[:, :]))
                        n_ea = 0
                        for q in range(4):
                            lo, hi = q * (T // 4), (q + 1) * (T // 4)
                            n_ea += 16 * len(by_edge(ea16, a["edge_attr_16"], lo, hi))
                            dve.wait_ge(s_ea, n_ea)
                            v_chain(dve, dve.tensor_tensor(ea16[:, :, :], ea16[:, :, :],
                                                           a_rows[:, 0:1, :].to_broadcast([P, T // 4, FIN]), ALU.mult))
                            dve.tensor_reduce(rec_d[:, lo:hi, 4], ea16[:, :, :], AX.X, ALU.add).then_inc(s_eafree, 1)
                            dve.wait_ge(s_eafree, q + 1)
                        for k, (key, rec, keep, last) in enumerate(((srct, rec_s, keep_s, last_s),
                                                                    (dstt, rec_d, keep_d, last_d))):
                            v_chain(dve, dve.tensor_scalar(ti, key[:, :], P - 1, None, ALU.bitwise_and))
                            v_chain(dve, dve.tensor_copy(rec[:, :, 0], ti))
                            v_chain(dve, dve.tensor_scalar(ti, key[:, :], 7, None, ALU.arith_shift_right))
                            v_chain(dve, dve.tensor_copy(blkf[:, :], ti))
                            for b in range(NB):
                                v_chain(dve, dve.tensor_scalar(onehot[:, :], blkf[:, :], float(b), 0.0, ALU.is_equal,
                                                               ALU.add, accum_out=cnt[:, b:b + 1]))
                            v_chain(dve, dve.tensor_copy(tot[:, :], cnt[:, :]))
                            dve.tensor_copy(first[:, :], cnt[:, :]).then_inc(s_cnt, 1)
                            dve.wait_ge(s_tri, k + 1)
                            v_chain(dve, dve.tensor_scalar(tot[:, :], banks[1][:, 0:NB], float(GE - 1), None, ALU.add))
                            v_chain(dve, dve.tensor_copy(toti[:, :], tot[:, :]))
                            v_chain(dve, dve.tensor_scalar(toti[:, :], toti[:, :], GE.bit_length() - 1, None, ALU.arith_shift_right))
                            v_chain(dve, dve.tensor_copy(tot[:, :], toti[:, :]))
                            v_chain(dve, dve.tensor_scalar(tot[:, :], tot[:, :], 1.0, None, ALU.max))
                            v_chain(dve, dve.tensor_tensor_scan(nxt[:, :], tot[:, :], tot[:, :], 0.0, ALU.add, ALU.bypass))
                            v_chain(dve, dve.tensor_tensor(first[:, :], nxt[:, :], tot[:, :], ALU.subtract))
                            v_chain(dve, dve.tensor_scalar(delta[:, :], first[:, :], float(GE), -1.0, ALU.mult, ALU.add))
                            v_chain(dve, dve.tensor_tensor(delta[:, :], delta[:, :], banks[0][:, 0:NB], ALU.add))
                            v_chain(dve, dve.tensor_scalar(tot[:, :], nxt[:, :], -1.0, float(P), ALU.add, ALU.mult))
                            v_chain(dve, dve.tensor_scalar(last[:, :], tot[:, :], iota_p[:, 0:1], None, ALU.add))
                            dve.wait_ge(s_const, 1)
                            v_chain(dve, dve.memset(accg[:, :], 1.0))
                            for b in range(NB):
                                v_chain(dve, dve.tensor_scalar(keep[:, :], iota_g[:, :], first[:, b:b + 1], -1.0, ALU.is_equal, ALU.mult))
                                v_chain(dve, dve.tensor_tensor(accg[:, :], accg[:, :], keep[:, :], ALU.add))
                            v_chain(dve, dve.tensor_copy(keep[:, :], accg[:, :]))
                            if k == 0:
                                v_chain(dve, dve.memset(accg[:, :], 0.0))
                                for b in range(NB - 1):
                                    v_chain(dve, dve.scalar_tensor_tensor(accg[:, :], iota_g[:, :], nxt[:, b:b + 1], accg[:, :], ALU.is_ge, ALU.add))
                                v_chain(dve, dve.memset(blk_s[:, :], 0))
                                v_chain(dve, dve.tensor_scalar(blk_s[:, 0:NG], accg[:, :], float(P), iota_p[:, 0:1], ALU.mult, ALU.add))
                            v_chain(dve, dve.memset(posf[:, :], -1.0))
                            for b in range(NB):
                                v_chain(dve, dve.tensor_scalar(onehot[:, :], blkf[:, :], float(b), None, ALU.is_equal))
                                v_chain(dve, dve.tensor_tensor_scan(run[:, :], onehot[:, :], onehot[:, :], delta[:, b:b + 1], ALU.add, ALU.bypass))
                                v_chain(dve, dve.copy_predicated(posf[:, :], onehot[:, :].bitcast(I32), run[:, :]))
                            v_chain(dve, dve.tensor_copy(ti, posf[:, :]))
                            v_chain(dve, dve.tensor_scalar(t8, ti, P - 1, None, ALU.bitwise_and))
                            v_chain(dve, dve.tensor_scalar(ti, ti, 7, None, ALU.arith_shift_right))
                            v_chain(dve, dve.scalar_tensor_tensor(pos_i[k][:, :], t8, float(NT), ti, ALU.mult, ALU.add))
                            v_chain(dve, dve.tensor_scalar(onehot[:, :], posf[:, :], 0.0, None, ALU.is_lt))
                            v_chain(dve, dve.memset(run[:, :], 1.0))
                            v_chain(dve, dve.tensor_tensor_scan(run[:, :], run[:, :], run[:, :], float(P * NT - 1), ALU.add, ALU.bypass))
                            v_chain(dve, dve.tensor_copy(t8, run[:, :]))
                            v_chain(dve, dve.copy_predicated(pos_i[k][:, :], onehot[:, :].bitcast(I32), t8))

            ring = sb("ring", [P, 2, 4, W], F32, st)
            rpos = sb("rpos", [P, 2, 4], I32, st)
            ring_ready = sem("ring_ready")
            for k, (rec, lst) in enumerate(((rec_s, list_s), (rec_d, list_d))):
                with nc.Block() as block:
                    @block.vector
                    def _(dve):
                        def fill(i, h, wait):
                            if wait:
                                dve.wait_ge(scattered[h], i * 64 + k * (T // 8) * 64)
                            dve.tensor_copy(ring[:, h, :, :], rec[:, bass.ds(i * 8 + h * 4, 4), :])
                            dve.tensor_copy(rpos[:, h, :], pos_i[k][:, bass.ds(i * 8 + h * 4, 4)]).then_inc(ring_ready, 1)

                        fill(0, 0, k > 0)
                        fill(0, 1, k > 0)
                        with dve.Fori(1, T // 8) as i:
                            fill(i, 0, True)
                            fill(i, 1, True)

                    @block.gpsimd
                    def _(pool):
                        with pool.Fori(0, T // 8) as i:
                            for h in range(2):
                                pool.wait_ge(ring_ready, i * 2 + h + 1 + k * (T // 8) * 2)
                                pool_gate(pool)
                                for j in range(4):
                                    pool.indirect_dma_start(lst[:, :], IndirectOffsetOnAxis(ap=rpos[:, h, j:j + 1], axis=0),
                                                            ring[:, h, j, :], None).then_inc(scattered[h], 16)
                        for h in range(2):
                            pool.wait_ge(scattered[h], (k + 1) * (T // 8) * 64)

        with ExitStack() as st:
            lt = sb("lt", [P, NT, W], F32, st)
            rowbuf = sb("rowbuf", [P, 5, 8, P], F32, st)
            s_l, s_take, s_tr, s_cp = sem("s_l"), sem("s_take"), sem("s_tr"), sem("s_cp")
            C8 = NT // 8
            with nc.Block() as block:
                @block.sync
                def _(sp):
                    sp.dma_start(lt[:, :, :].rearrange("p t w -> p (t w)"),
                                 list_s[0:P * NT, :].rearrange("(p t) w -> p (t w)", p=P)).then_inc(s_l, 16)
                    sp.wait_ge(s_take, 1)
                    sp.wait_ge(s_tr, 10)
                    sp.dma_start(lt[:, :, :].rearrange("p t w -> p (t w)"),
                                 list_d[0:P * NT, :].rearrange("(p t) w -> p (t w)", p=P)).then_inc(s_l, 16)
                    sp.wait_ge(s_cp, 10)
                    for r in range(5):
                        sp_dma(sp, sp.dma_start(rows_s[r, :].rearrange("(c t p) -> t c p", c=8, p=P), rowbuf[0:C8, r, :, :]), 16)

                @block.tensor
                def _(pe):
                    pe.wait_ge(s_l, 16)
                    for r in range(5):
                        w = (0, 3, 4, 5, 6)[r]
                        for hf in range(2):
                            n = 2 * r + hf
                            if n >= 2:
                                pe.wait_ge(s_cp, n - 1)
                            for c in range(4):
                                m = pe.transpose(banks[n % 2][0:C8, c * P:(c + 1) * P],
                                                 lt[:, (4 * hf + c) * C8:(4 * hf + c + 1) * C8, w], ident[:, :])
                            m.then_inc(s_tr, 1)

                @block.vector
                def _(dve):
                    dve.wait_ge(s_l, 16)
                    dve.tensor_copy(loc_s[:, :], lt[:, :, 0])
                    dve.tensor_copy(col_s[:, 0:NT], lt[:, :, 1].bitcast(I32))
                    dve.tensor_copy(w_s[:, :], lt[:, :, 2]).then_inc(s_take, 1)
                    for n in range(10):
                        dve.wait_ge(s_tr, n + 1)
                        dve.tensor_copy(rowbuf[0:C8, n // 2, 4 * (n % 2):4 * (n % 2) + 4, :],
                                        banks[n % 2][0:C8, :].rearrange("t (c p) -> t c p", c=4)).then_inc(s_cp, 1)
                    dve.wait_ge(s_l, 32)
                    dve.tensor_copy(loc_d[:, :], lt[:, :, 0])
                    dve.tensor_copy(src_d[:, 0:NT], lt[:, :, 1].bitcast(I32))
                    dve.tensor_copy(rel_d[:, 0:NT], lt[:, :, 2].bitcast(I32))
                    dve.tensor_copy(typ_d[:, :], lt[:, :, 3])
                    v_chain(dve, dve.tensor_copy(hea_d[:, :], lt[:, :, 4]))

        def moved(k, h, by):
            d, slot = divmod(h + by, U)
            return (k + d if d else k), slot

        def there(k, h, lag=0):
            return not isinstance(k, int) or lag <= k * U + h < NG

        def turns(eng, step):
            for k in (0, 1):
                for h in range(U):
                    step(k, h)
            with eng.Fori(2, K - 1) as k:
                for h in range(U):
                    step(k, h)
            for h in range(U):
                step(K - 1, h)

        d_idx, d_rhs, d_sum, d_acc, d_part = (sem("d_" + n) for n in ("idx", "rhs", "sum", "acc", "part"))
        d_got = [sem(f"d_got{h}") for h in range(U)]
        d_stored = [sem(f"d_stored{h}") for h in range(U)]
        passes, parted = [0], [0]

        def dst_pass(mode, table, idx_all, f, agg):
            width = dict(plain=f, msg=32, types=NTYPE * f + NTYPE, types_only=NTYPE * f)[mode]
            store = agg_d[width]
            typed = mode.startswith("types")
            turn = passes[0]
            passes[0] += 1
            g0, k0 = turn * NG, turn * K
            pt0 = parted[0]
            if mode != "plain":
                parted[0] += NG
            with ExitStack() as st:
                idx = sb(f"idx{turn}", [P, U, G], I32, st)
                got = sb(f"got{turn}", [P, U, G, f], F32, st)
                oh = sb(f"oh{turn}", [P, U, G, P], F32, st)
                rhs = got if mode == "plain" else sb(f"rhs{turn}", [P, U, G, width], F32, st)
                gate = sb(f"gate{turn}", [P, U, G], F32, st)
                oh8 = sb(f"oh8{turn}", [P, U, G, NTYPE], F32, st)
                acc = sb(f"acc{turn}", [P, U, width], F32, st)
                with nc.Block() as block:
                    @block.gpsimd
                    def _(pool):
                        def gather(k, h):
                            n = k * U + h
                            if there(k, h, U):
                                pool.wait_ge(d_sum if mode == "plain" else d_rhs, g0 + n - U + 1)
                            pool.wait_ge(d_idx, g0 + n + 1)
                            pool_gate(pool)
                            for j in range(G):
                                pool.indirect_dma_start(got[:, h, j, :], None, table,
                                                        IndirectOffsetOnAxis(ap=idx[:, h, j:j + 1], axis=0)).then_inc(d_got[h], 16)
                        turns(pool, gather)
                        for h in range(U):
                            pool.wait_ge(d_stored[h], 16 * (k0 + K))
                        for b in range(NB):
                            pool.indirect_dma_start(agg[:, b, :], None, store,
                                                    IndirectOffsetOnAxis(ap=last_d[:, b:b + 1], axis=0)).then_inc(pool_dma.sem, 16)
                        pool_dma.n += 16 * NB
                        pool.wait_ge(pool_dma.sem, pool_dma.n)

                    @block.sync
                    def _(sp):
                        def save_sum(k, h):
                            sp.wait_ge(d_acc, g0 + k * U + h + 1)
                            sp.dma_start(store[bass.ds((k * U + h) * P, P), :], acc[:, h, :]).then_inc(d_stored[h], 16)
                        turns(sp, save_sum)

                    @block.tensor
                    def _(pe):
                        def sums(k, h):
                            n = k * U + h
                            if there(k, h, U):
                                pe.wait_ge(d_acc, g0 + n - U + 1)
                            if mode == "plain":
                                pe.wait_ge(d_got[h], 16 * G * (k0 + k + 1))
                            pe.wait_ge(d_rhs, g0 + n + 1)
                            for j in range(G):
                                m = pe.matmul(banks[h][:, 0:width], oh[:, h, j, :], rhs[:, h, j, :], start=(j == 0), stop=(j == G - 1))
                            m.then_inc(d_sum, 1)
                        turns(pe, sums)

                    @block.vector
                    def _(dve):
                        def indices(k, h):
                            if not there(k, h):
                                return
                            if there(k, h, U):
                                dve.wait_ge(d_got[h], 16 * G * (k0 + k))
                            dve.tensor_copy(idx[:, h, :], idx_all[:, bass.ds((k * U + h) * G, G)]).then_inc(d_idx, 1)

                        def build(k, h):
                            n = k * U + h
                            if there(k, h, U):
                                dve.wait_ge(d_sum, g0 + n - U + 1)
                            ins = dve.tensor_tensor(oh[:, h, :, :], iota_row[:, None, :].to_broadcast([P, G, P]),
                                                    loc_d[:, bass.ds(n * G, G)][:, :, None].to_broadcast([P, G, P]), ALU.is_equal)
                            if mode == "plain":
                                ins.then_inc(d_rhs, 1)
                                return
                            if typed:
                                dve.tensor_tensor(oh8[:, h, :, :], iota8[:, None, :].to_broadcast([P, G, NTYPE]),
                                                  typ_d[:, bass.ds(n * G, G)][:, :, None].to_broadcast([P, G, NTYPE]),
                                                  ALU.is_equal).then_inc(d_part, 1)
                                dve.wait_ge(d_part, pt0 + n + 1)
                                if mode == "types":
                                    dve.tensor_copy(rhs[:, h, :, NTYPE * f:width], oh8[:, h, :, :])
                                dve.wait_ge(d_got[h], 16 * G * (k0 + k + 1))
                                for j in range(G):
                                    ins = dve.tensor_tensor(
                                        rhs[:, h, j, 0:NTYPE * f].rearrange("p (r f) -> p r f", r=NTYPE),
                                        got[:, h, j, None, :].to_broadcast([P, NTYPE, f]),
                                        oh8[:, h, j, :, None].to_broadcast([P, NTYPE, f]), ALU.mult)
                                ins.then_inc(d_rhs, 1)
                                return
                            dve.wait_ge(d_got[h], 16 * G * (k0 + k + 1))
                            dve.tensor_copy(rhs[:, h, :, 16:32], got[:, h, :, 0:16])
                            dve.tensor_tensor(gate[:, h, :], got[:, h, :, 16], hea_d[:, bass.ds(n * G, G)], ALU.add).then_inc(d_part, 1)
                            dve.wait_ge(d_part, pt0 + n + 1)
                            dve.tensor_tensor(rhs[:, h, :, 0:16], got[:, h, :, 0:16],
                                              gate[:, h, :, None].to_broadcast([P, G, 16]), ALU.mult).then_inc(d_rhs, 1)

                        def add(k, h):
                            n = k * U + h
                            dve.wait_ge(d_sum, g0 + n + 1)
                            if there(k, h, U):
                                dve.wait_ge(d_stored[h], 16 * (k0 + k))
                            if there(k, h, 1):
                                dve.wait_ge(d_acc, g0 + n)
                            dve.scalar_tensor_tensor(acc[:, h, :], acc[:, (h - 1) % U, :], keep_d[:, bass.ds(n, 1)],
                                                     banks[h][:, 0:width], ALU.mult, ALU.add).then_inc(d_acc, 1)

                        def step(k, h):
                            indices(*moved(k, h, U - 1))
                            build(k, h)
                            if there(k, h, 2):
                                add(*moved(k, h, -2))

                        v_chain(dve, dve.memset(acc[:, U - 1, :], 0.0))
                        for h in range(U - 1):
                            indices(0, h)
                        turns(dve, step)
                        add(K - 1, U - 2)
                        add(K - 1, U - 1)

        def turn_block(src, f, dst, extra=None):
            b_tr, b_cp = from_pe.base(len(CH)), to_pe.base(len(CH))
            with nc.Block() as block:
                @block.tensor
                def _(pe):
                    for c, (at, n) in enumerate(CH):
                        if c >= 2:
                            pe.wait_ge(to_pe.sem, b_cp + c - 1)
                        for j in range(n // P):
                            m = pe.transpose(banks[c % 2][0:f, j * P:(j + 1) * P], src[:, at // P + j, :], ident[:, :])
                        m.then_inc(from_pe.sem, 1)

                @block.vector
                def _(dve):
                    for c, (at, n) in enumerate(CH):
                        dve.wait_ge(from_pe.sem, b_tr + c + 1)
                        dve.tensor_copy(dst[0:f, at:at + n], banks[c % 2][0:f, 0:n]).then_inc(to_pe.sem, 1)

        def features(ws_, ins_, dst, m_, func, bias, add_to=None, mask=None):
            b_mm, b_ev = from_pe.base(len(CH)), from_act.base(len(CH))
            with nc.Block() as block:
                @block.tensor
                def _(pe):
                    for c, (at, n) in enumerate(CH):
                        if c >= 2:
                            pe.wait_ge(from_act.sem, b_ev + c - 1)
                        for q, (w_, i_) in enumerate(zip(ws_, ins_)):
                            m = pe.matmul(banks[c % 2][0:m_, 0:n], w_, i_[:, at:at + n], start=(q == 0), stop=(q == len(ws_) - 1))
                        m.then_inc(from_pe.sem, 1)

                @block.scalar
                def _(act):
                    for c, (at, n) in enumerate(CH):
                        act.wait_ge(from_pe.sem, b_mm + c + 1)
                        act.activation(dst[0:m_, at:at + n], banks[c % 2][0:m_, 0:n], func, bias=bias).then_inc(from_act.sem, 1)

                @block.vector
                def _(dve):
                    for c, (at, n) in enumerate(CH):
                        if add_to is None:
                            break
                        dve.wait_ge(from_act.sem, b_ev + c + 1)
                        v_chain(dve, dve.tensor_tensor(dst[:, at:at + n], dst[:, at:at + n], add_to[:, at:at + n], ALU.add))
                        dve.tensor_tensor(add_to[:, at:at + n], dst[:, at:at + n], mask[:, at:at + n], ALU.mult)

        def nodes(pairs, m_, bank):
            with nc.Block() as block:
                @block.tensor
                def _(pe):
                    for b in range(NB):
                        for q, (i_, w_) in enumerate(pairs):
                            pe.matmul(banks[bank][:, b * m_:(b + 1) * m_], i_[:, b * P:(b + 1) * P], w_,
                                      start=(q == 0), stop=(q == len(pairs) - 1))

        def row(t, f=FIN):
            return t[:, None, :].to_broadcast([P, NB, f])

        def each(t, f=FIN):
            return t[:, :, None].to_broadcast([P, NB, f])

        def layernorm(dve, b_act):
            mean, var, r = stat[:, 0, :], stat[:, 1, :], stat[:, 2, :]
            v_chain(dve, dve.tensor_reduce(mean, x[:, :, :], AX.X, ALU.add))
            v_chain(dve, dve.tensor_scalar(mean, mean, 1.0 / FIN, None, ALU.mult))
            v_chain(dve, dve.tensor_tensor(x[:, :, :], x[:, :, :], each(mean), ALU.subtract))
            v_chain(dve, dve.tensor_tensor(tmp[:, :, :], x[:, :, :], x[:, :, :], ALU.mult))
            v_chain(dve, dve.tensor_reduce(var, tmp[:, :, :], AX.X, ALU.add))
            dve.tensor_scalar(var, var, 1.0 / FIN, EPS, ALU.mult, ALU.add).then_inc(to_act.sem, 1)
            dve.wait_ge(from_act.sem, b_act + 1)
            v_chain(dve, dve.reciprocal(r, r))
            v_chain(dve, dve.tensor_tensor(x[:, :, :], x[:, :, :], each(r), ALU.mult))

        def root_step(act, b_to):
            act.wait_ge(to_act.sem, b_to + 1)
            act.activation(stat[:, 2, :], stat[:, 1, :], ACT.Sqrt).then_inc(from_act.sem, 1)

        def load(pairs):
            with nc.Block() as block:
                @block.sync
                def _(sp):
                    with nc.allow_non_contiguous_dma(reason="small weights"):
                        for d, s_ in pairs:
                            sp.dma_start(d, s_).then_inc(sp_dma.sem, 16)
                            sp_dma.n += 16
                    sp.wait_ge(sp_dma.sem, sp_dma.n)

        def save(pairs):
            load(pairs)

        def column(v):
            return v.rearrange("(p a) -> p a", a=1)

        def spread(v, n):
            return v.rearrange("(a n) -> a n", a=1).to_broadcast([P, n])

        with ExitStack() as st:
            w1a, w1b = sb("w1a", [16, 16], F32, st), sb("w1b", [16, 16], F32, st)
            w2a, w2b = sb("w2a", [16, 16], F32, st), sb("w2b", [16, 16], F32, st)
            b1a, b2a = sb("b1a", [16, 1], F32, st), sb("b2a", [16, 1], F32, st)
            b1b, b2b = sb("b1b", [P, 16], F32, st), sb("b2b", [P, 16], F32, st)
            eps = sb("eps", [P, 2], F32, st)
            h = sb("h", [P, NB, FIN], F32, st)
            agg = sb("agg0", [P, NB, FIN], F32, st)
            hT = sb("hT", [FIN, NP], F32, st)
            h1T = sb("h1T", [FIN, NP], F32, st)
            load([(w1a[:, :], a["L0_gnn_w1a"]), (w1b[:, :], a["L0_gnn_w1b"]), (w2a[:, :], a["L0_gnn_w2a"]),
                  (w2b[:, :], a["L0_gnn_w2b"]), (b1a[:, :], column(a["L0_gnn_b1a"])), (b2a[:, :], column(a["L0_gnn_b2a"])),
                  (b1b[:, :], spread(a["L0_gnn_b1b"], 16)), (b2b[:, :], spread(a["L0_gnn_b2b"], 16)),
                  (eps[:, 0:1], a["L0_gnn_eps1"].to_broadcast([P, 1])), (eps[:, 1:2], a["L0_gnn_eps2"].to_broadcast([P, 1]))])
            for layer, (wa_, ba_, wb_, bb_) in enumerate(((w1a, b1a, w1b, b1b), (w2a, b2a, w2b, b2b))):
                h_in = x if layer == 0 else h
                dst_pass("plain", x_tab if layer == 0 else h_tab, src_d, FIN, agg)
                with nc.Block() as block:
                    @block.vector
                    def _(dve):
                        if layer == 0:
                            v_chain(dve, dve.tensor_scalar(eps[:, :], eps[:, :], 1.0, None, ALU.add))
                        v_chain(dve, dve.scalar_tensor_tensor(agg[:, :, :], h_in[:, :, :], eps[:, layer:layer + 1],
                                                              agg[:, :, :], ALU.mult, ALU.add))
                turn_block(agg, FIN, hT)
                features([wa_[:, :]], [hT], h1T, FIN, ACT.Relu, ba_[:, 0:1])
                nodes([(h1T, wb_[:, :])], FIN, 0)
                out0 = banks[0][:, 0:NB * FIN].rearrange("p (b f) -> p b f", b=NB)
                if layer == 0:
                    with nc.Block() as block:
                        @block.vector
                        def _(dve):
                            v_chain(dve, dve.tensor_tensor(h[:, :, :], out0, row(bb_), ALU.add))
                            v_chain(dve, dve.tensor_scalar(h[:, :, :], h[:, :, :], 0.0, None, ALU.max))
                    save([(h_tab.rearrange("(b p) f -> p b f", p=P), h[:, :, :])])
                    continue
                b_to, b_fr = to_act.base(3), from_act.base(3)
                with nc.Block() as block:
                    @block.vector
                    def _(dve):
                        mx, sm = stat[:, 0, :], stat[:, 1, :]
                        v_chain(dve, dve.tensor_tensor(h[:, :, :], out0, row(bb_), ALU.add))
                        v_chain(dve, dve.tensor_reduce(mx, h[:, :, :], AX.X, ALU.max))
                        dve.tensor_tensor(h[:, :, :], h[:, :, :], each(mx), ALU.subtract).then_inc(to_act.sem, 1)
                        dve.wait_ge(from_act.sem, b_fr + 1)
                        dve.tensor_reduce(sm, tmp[:, :, :], AX.X, ALU.add).then_inc(to_act.sem, 1)
                        dve.wait_ge(from_act.sem, b_fr + 2)
                        v_chain(dve, dve.tensor_tensor(h[:, :, :], h[:, :, :], each(stat[:, 2, :]), ALU.subtract))
                        v_chain(dve, dve.tensor_tensor(x[:, :, :], x[:, :, :], h[:, :, :], ALU.add))
                        layernorm(dve, b_fr + 2)

                    @block.scalar
                    def _(act):
                        act.wait_ge(to_act.sem, b_to + 1)
                        act.activation(tmp[:, :, :], h[:, :, :], ACT.Exp).then_inc(from_act.sem, 1)
                        act.wait_ge(to_act.sem, b_to + 2)
                        act.activation(stat[:, 2, :], stat[:, 1, :], ACT.Ln).then_inc(from_act.sem, 1)
                        root_step(act, b_to + 2)

        m_idx, m_oht, m_ohm, m_z1, m_h1, m_z2, m_z2b, m_h2, m_sum, m_acc = (
            sem("m_" + n) for n in ("idx", "oht", "ohm", "z1", "h1", "z2", "z2b", "h2", "sum", "acc"))
        m_got, m_ld, m_stored = ([sem(f"m_{n}{h}") for h in range(U)] for n in ("got", "ld", "stored"))

        def edge_mlp(layer, we, w2, b1, b2, agg):
            g0, k0 = layer * NG, layer * K
            with ExitStack() as st:
                qidx = sb(f"qidx{layer}", [P, U, G], I32, st)
                qg = sb(f"qg{layer}", [P, U, G, HID], F32, st)
                pb = sb(f"pb{layer}", [P, U, HID], F32, st)
                places = sb(f"places{layer}", [P, U, GE], F32, st)
                eat = sb(f"eat{layer}", [4, U, GE], F32, st)
                oht = sb(f"oht{layer}", [P, U, GE], F32, st)
                ohm = sb(f"ohm{layer}", [P, 2, G, P], F32, st)
                h1 = sb(f"h1{layer}", [P, 2, GE], F32, st)
                z2b = sb(f"z2b{layer}", [P, 2, G, HID], F32, st)
                h2 = sb(f"h2{layer}", [P, 2, G, HID], F32, st)
                acc = sb(f"macc{layer}", [P, U, HID], F32, st)

                with nc.Block() as block:
                    @block.gpsimd
                    def _(pool):
                        def gather(k, h):
                            n = k * U + h
                            if there(k, h, U):
                                pool.wait_ge(m_z1, g0 + n - U + 1)
                            pool.wait_ge(m_idx, g0 + n + 1)
                            pool_gate(pool)
                            for j in range(G):
                                pool.indirect_dma_start(qg[:, h, j, :], None, q_tab,
                                                        IndirectOffsetOnAxis(ap=qidx[:, h, j:j + 1], axis=0)).then_inc(m_got[h], 16)
                        turns(pool, gather)
                        for h in range(U):
                            pool.wait_ge(m_stored[h], 16 * (k0 + K))
                        for b in range(NB):
                            pool.indirect_dma_start(agg[:, b, :], None, agg_s,
                                                    IndirectOffsetOnAxis(ap=last_s[:, b:b + 1], axis=0)).then_inc(pool_dma.sem, 16)
                        pool_dma.n += 16 * NB
                        pool.wait_ge(pool_dma.sem, pool_dma.n)

                    @block.sync
                    def _(sp):
                        def fetch(k, h):
                            n = k * U + h
                            if there(k, h, U):
                                sp.wait_ge(m_z1, g0 + n - U + 1)
                                sp.wait_ge(m_oht, g0 + n - U + 1)
                            sp.dma_start(places[:, h, :], rows_s[0:1, bass.ds(n * GE, GE)].to_broadcast([P, GE])).then_inc(m_ld[h], 16)
                            sp.dma_start(eat[:, h, :], rows_s[1:5, bass.ds(n * GE, GE)]).then_inc(m_ld[h], 16)
                            row = sp.value_load(blk_s[0:1, bass.ds(n, 1)], min_val=0, max_val=NP - P)
                            sp.dma_start(pb[:, h, :], p_tab[bass.ds(row, P), :]).then_inc(m_ld[h], 16)
                        turns(sp, fetch)

                    @block.tensor
                    def _(pe):
                        def first(k, h):
                            n = k * U + h
                            if there(k, h, 2):
                                pe.wait_ge(m_h1, g0 + n - 1)
                            pe.wait_ge(m_ld[h], 48 * (k0 + k + 1))
                            pe.wait_ge(m_oht, g0 + n + 1)
                            z1 = banks[h % 2][:, 0:GE]
                            pe.matmul(z1[:, :], pb[:, h, :], oht[:, h, :], start=True, stop=False)
                            pe.matmul(z1[:, :], we, eat[:, h, :], start=False, stop=False)
                            pe.wait_ge(m_got[h], 16 * G * (k0 + k + 1))
                            for j in range(G):
                                m = pe.matmul(z1[:, j * P:(j + 1) * P], qg[:, h, j, :], ident[:, :], start=False, stop=(j == G - 1))
                            m.then_inc(m_z1, 1)

                        def second(k, h):
                            n = k * U + h
                            if there(k, h, 2):
                                pe.wait_ge(m_z2b, g0 + n - 1)
                            pe.wait_ge(m_h1, g0 + n + 1)
                            for j in range(G):
                                m = pe.matmul(banks[2 + h % 2][:, j * P:(j + 1) * P], h1[:, h % 2, j * P:(j + 1) * P], w2, start=True, stop=True)
                            m.then_inc(m_z2, 1)

                        def sums(k, h):
                            n = k * U + h
                            if there(k, h, 2):
                                pe.wait_ge(m_acc, g0 + n - 1)
                            pe.wait_ge(m_ohm, g0 + n + 1)
                            pe.wait_ge(m_h2, g0 + n + 1)
                            for j in range(G):
                                m = pe.matmul(banks[4 + h % 2][:, 0:HID], ohm[:, h % 2, j, :], h2[:, h % 2, j, :], start=(j == 0), stop=(j == G - 1))
                            m.then_inc(m_sum, 1)

                        def step(k, h):
                            first(k, h)
                            if there(k, h, 1):
                                second(*moved(k, h, -1))
                            if there(k, h, 2):
                                sums(*moved(k, h, -2))
                        turns(pe, step)
                        second(K - 1, U - 1)
                        sums(K - 1, U - 2)
                        sums(K - 1, U - 1)

                    @block.scalar
                    def _(act):
                        def one(k, h):
                            n = k * U + h
                            if there(k, h, 2):
                                act.wait_ge(m_z2, g0 + n - 1)
                            act.wait_ge(m_z1, g0 + n + 1)
                            act.activation(h1[:, h % 2, :], banks[h % 2][:, 0:GE], ACT.Silu, bias=b1).then_inc(m_h1, 1)

                        def two(k, h):
                            n = k * U + h
                            if there(k, h, 2):
                                act.wait_ge(m_sum, g0 + n - 1)
                            act.wait_ge(m_z2b, g0 + n + 1)
                            act.activation(h2[:, h % 2, :, :], z2b[:, h % 2, :, :], ACT.Silu).then_inc(m_h2, 1)

                        def save_sum(k, h):
                            act.wait_ge(m_acc, g0 + k * U + h + 1)
                            act.dma_start(agg_s[bass.ds((k * U + h) * P, P), :], acc[:, h, :]).then_inc(m_stored[h], 16)

                        def step(k, h):
                            one(k, h)
                            if there(k, h, 1):
                                two(*moved(k, h, -1))
                            if there(k, h, 3):
                                save_sum(*moved(k, h, -3))
                        turns(act, step)
                        two(K - 1, U - 1)
                        for h in range(U - 3, U):
                            save_sum(K - 1, h)

                    @block.vector
                    def _(dve):
                        def indices(k, h):
                            if not there(k, h):
                                return
                            if there(k, h, U):
                                dve.wait_ge(m_got[h], 16 * G * (k0 + k))
                            dve.tensor_copy(qidx[:, h, :], col_s[:, bass.ds((k * U + h) * G, G)]).then_inc(m_idx, 1)

                        def build(k, h):
                            if not there(k, h):
                                return
                            if there(k, h, U):
                                dve.wait_ge(m_z1, g0 + k * U + h - U + 1)
                            dve.wait_ge(m_ld[h], 48 * (k0 + k + 1))
                            dve.tensor_scalar(oht[:, h, :], places[:, h, :], iota_p[:, 0:1], None, ALU.is_equal).then_inc(m_oht, 1)

                        def build_m(k, h):
                            n = k * U + h
                            if there(k, h, 2):
                                dve.wait_ge(m_sum, g0 + n - 1)
                            for j in range(G):
                                t = n * G + j
                                m = dve.tensor_scalar(ohm[:, h % 2, j, :], iota_row[:, :], loc_s[:, bass.ds(t, 1)],
                                                      w_s[:, bass.ds(t, 1)], ALU.is_equal, ALU.mult)
                            m.then_inc(m_ohm, 1)

                        def bias(k, h):
                            n = k * U + h
                            if there(k, h, 2):
                                dve.wait_ge(m_h2, g0 + n - 1)
                            dve.wait_ge(m_z2, g0 + n + 1)
                            dve.tensor_tensor(z2b[:, h % 2, :, :], banks[2 + h % 2][:, 0:GE].rearrange("p (j f) -> p j f", j=G),
                                              b2[:, None, :].to_broadcast([P, G, HID]), ALU.add).then_inc(m_z2b, 1)

                        def add(k, h):
                            n = k * U + h
                            if there(k, h, U):
                                dve.wait_ge(m_stored[h], 16 * (k0 + k))
                            if there(k, h, 1):
                                dve.wait_ge(m_acc, g0 + n)
                            dve.wait_ge(m_sum, g0 + n + 1)
                            dve.scalar_tensor_tensor(acc[:, h, :], acc[:, (h - 1) % U, :], keep_s[:, bass.ds(n, 1)],
                                                     banks[4 + h % 2][:, 0:HID], ALU.mult, ALU.add).then_inc(m_acc, 1)

                        def step(k, h):
                            indices(*moved(k, h, U - 1))
                            build(*moved(k, h, 1))
                            if there(k, h, 1):
                                build_m(*moved(k, h, -1))
                                bias(*moved(k, h, -1))
                            if there(k, h, 2):
                                add(*moved(k, h, -2))

                        v_chain(dve, dve.memset(acc[:, U - 1, :], 0.0))
                        for h in range(U - 1):
                            indices(0, h)
                        build(0, 0)
                        turns(dve, step)
                        build_m(K - 1, U - 1)
                        bias(K - 1, U - 1)
                        add(K - 1, U - 2)
                        add(K - 1, U - 1)

        with ExitStack() as st:
            hT = sb("hidT", [P, NP], F32, st)
            aggT = sb("aggT", [P, NP], F32, st)
            nT = sb("nT", [P, NP], F32, st)
            maskT = sb("maskT", [P, NP], F32, st)
            agg = sb("agg1", [P, NB, HID], F32, st)
            wpq = sb("wpq", [P, 2, HID], F32, st)
            pq = sb("pq", [P, 2, 2, HID], F32, st)
            we = sb("we", [4, HID], F32, st)
            w2 = sb("w2", [P, HID], F32, st)
            b1, b2 = sb("b1", [P, 1], F32, st), sb("b2", [P, HID], F32, st)
            wn1 = sb("wn1", [P, 2, HID], F32, st)
            wn2 = sb("wn2", [P, HID], F32, st)
            bn1, bn2 = sb("bn1", [P, 1], F32, st), sb("bn2", [P, 1], F32, st)
            wemb, bemb = sb("wemb", [FIN, HID], F32, st), sb("bemb", [P, 1], F32, st)
            wout, bout = sb("wout", [P, FIN], F32, st), sb("bout", [P, FIN], F32, st)
            pq_out = [sem("pq_out0"), sem("pq_out1")]
            pq_n = [0, 0]

            with nc.Block() as block:
                @block.vector
                def _(dve):
                    v_chain(dve, dve.memset(maskT[:, :], 0.0))
            load([(maskT[:, 0:N], a["node_vec1"].rearrange("n a -> a n").to_broadcast([P, N])),
                  (wemb[:, :], a["L1_gnn_emb_w"]), (bemb[:, :], column(a["L1_gnn_emb_b"])),
                  (wout[:, :], a["L1_gnn_out_w"]), (bout[:, :], spread(a["L1_gnn_out_b"], FIN))])
            turn_block(x, FIN, xT)
            features([wemb[:, :]], [xT], hT, HID, ACT.Identity, bemb[:, 0:1])
            for layer in range(L):
                ew1 = a["L1_gnn_edge_w1"][layer]
                nw1 = a["L1_gnn_node_w1"][layer]
                load([(wpq[:, 0, :], ew1[0:HID, :]), (wpq[:, 1, :], ew1[HID:2 * HID, :]), (we[:, :], ew1[2 * HID:2 * HID + 4, :]),
                      (b1[:, :], column(a["L1_gnn_edge_b1"][layer])), (w2[:, :], a["L1_gnn_edge_w2"][layer]),
                      (b2[:, :], spread(a["L1_gnn_edge_b2"][layer], HID)),
                      (wn1[:, 0, :], nw1[0:HID, :]), (wn1[:, 1, :], nw1[HID:2 * HID, :]),
                      (bn1[:, :], column(a["L1_gnn_node_b1"][layer])), (wn2[:, :], a["L1_gnn_node_w2"][layer]),
                      (bn2[:, :], column(a["L1_gnn_node_b2"][layer]))])
                b_mm, b_cp = from_pe.base(NB), to_pe.base(NB)
                with nc.Block() as block:
                    @block.tensor
                    def _(pe):
                        for b in range(NB):
                            if b >= 2:
                                pe.wait_ge(to_pe.sem, b_cp + b - 1)
                            pe.matmul(banks[b % 2][:, 0:2 * HID], hT[:, b * P:(b + 1) * P],
                                      wpq[:, :, :].rearrange("p k f -> p (k f)"), start=True, stop=True).then_inc(from_pe.sem, 1)

                    @block.vector
                    def _(dve):
                        for b in range(NB):
                            dve.wait_ge(from_pe.sem, b_mm + b + 1)
                            if pq_n[b % 2] > 0:
                                dve.wait_ge(pq_out[b % 2], pq_n[b % 2])
                            dve.tensor_copy(pq[:, b % 2, :, :], banks[b % 2][:, 0:2 * HID].rearrange("p (k f) -> p k f", k=2)).then_inc(to_pe.sem, 1)
                            pq_n[b % 2] += 32
                    @block.sync
                    def _(sp):
                        for b in range(NB):
                            sp.wait_ge(to_pe.sem, b_cp + b + 1)
                            sp.dma_start(p_tab[b * P:(b + 1) * P, :], pq[:, b % 2, 0, :]).then_inc(pq_out[b % 2], 16)
                            sp.dma_start(q_tab[b * P:(b + 1) * P, :], pq[:, b % 2, 1, :]).then_inc(pq_out[b % 2], 16)
                        for h in range(2):
                            sp.wait_ge(pq_out[h], pq_n[h])
                edge_mlp(layer, we[:, :], w2[:, :], b1[:, 0:1], b2, agg)
                turn_block(agg, HID, aggT)
                features([wn1[:, 0, :], wn1[:, 1, :]], [hT, aggT], nT, HID, ACT.Silu, bn1[:, 0:1])
                features([wn2[:, :]], [nT], aggT, HID, ACT.Identity, bn2[:, 0:1], add_to=hT, mask=maskT)
            nodes([(hT, wout[:, :])], FIN, 0)
            b_to, b_fr = to_act.base(1), from_act.base(1)
            with nc.Block() as block:
                @block.vector
                def _(dve):
                    o = banks[0][:, 0:NB * FIN].rearrange("p (b f) -> p b f", b=NB)
                    v_chain(dve, dve.tensor_tensor(tmp[:, :, :], o, row(bout), ALU.add))
                    v_chain(dve, dve.tensor_tensor(tmp[:, :, :], tmp[:, :, :], each(nodev), ALU.mult))
                    v_chain(dve, dve.tensor_tensor(x[:, :, :], x[:, :, :], tmp[:, :, :], ALU.add))
                    layernorm(dve, b_fr)

                @block.scalar
                def _(act):
                    root_step(act, b_to)

        with ExitStack() as st:
            wcT = sb("wcT", [NBAS, NREL], F32, st)
            vv = sb("vv", [NBAS, 16, 16], F32, st)
            gg = sb("gg", [NREL, 16, 16], F32, st)
            wr = sb("wr", [FIN, NREL, 17], F32, st)
            yb = sb("yb", [P, 2, NREL * 17], F32, st)
            wl = sb("wl", [FIN, NREL, 16], F32, st)
            agg = sb("agg2", [P, NB, 32], F32, st)
            s3 = sb("s3", [P, NB], F32, st)
            y_out = [sem("y_out0"), sem("y_out1")]
            load([(wcT[:, :], a["L2_gnn_w_comp"].rearrange("r b -> b r")),
                  (vv[:, :, :], a["L2_gnn_weight"].rearrange("b i o -> (b i o)").rearrange("(i b o) -> b i o", i=16, b=NBAS))])
            with nc.Block() as block:
                @block.tensor
                def _(pe):
                    pe.matmul(banks[0][0:NREL, 0:256], wcT[:, :], vv[:, :, :].rearrange("b i o -> b (i o)"), start=True, stop=True)
            with nc.Block() as block:
                @block.vector
                def _(dve):
                    v_chain(dve, dve.tensor_copy(gg[:, :, :], banks[0][0:NREL, 0:256].rearrange("r (i o) -> r i o", i=16)))
            save([(g_tab.rearrange("(i r o) -> r i o", i=16, r=NREL), gg[:, :, :])])
            load([(wl[:, :, :], g_tab.rearrange("(r i o) -> i r o", r=NREL, i=16))])
            turn_block(x, FIN, xT)
            b_mm, b_cp = from_pe.base(NB * 3), to_pe.base(NB * 3)
            with nc.Block() as block:
                @block.vector
                def _(dve):
                    v_chain(dve, dve.tensor_copy(wr[:, :, 0:16], wl[:, :, :]))
                    v_chain(dve, dve.tensor_copy(wr[:, :, 16:17], a_cols[:, None, 0:1].to_broadcast([FIN, NREL, 1])))
                    v_chain(dve, dve.tensor_tensor(tmp[:, :, :], x[:, :, :], a_rows[:, 1:2, :].to_broadcast([P, NB, FIN]), ALU.mult))
                    v_chain(dve, dve.tensor_reduce(s3[:, :], tmp[:, :, :], AX.X, ALU.add))
            YC = NREL * 17 // 3
            with nc.Block() as block:
                @block.tensor
                def _(pe):
                    for b in range(NB):
                        for c in range(3):
                            n = 3 * b + c
                            if n >= 6:
                                pe.wait_ge(to_pe.sem, b_cp + n - 5)
                            pe.matmul(banks[n % 6][:, 0:YC], xT[:, b * P:(b + 1) * P],
                                      wr[:, :, :].rearrange("i r o -> i (r o)")[:, c * YC:(c + 1) * YC], start=True, stop=True).then_inc(from_pe.sem, 1)

                @block.vector
                def _(dve):
                    for b in range(NB):
                        if b >= 2:
                            dve.wait_ge(y_out[b % 2], 16 * (b // 2))
                        for c in range(3):
                            n = 3 * b + c
                            dve.wait_ge(from_pe.sem, b_mm + n + 1)
                            dve.tensor_copy(yb[:, b % 2, c * YC:(c + 1) * YC], banks[n % 6][:, 0:YC]).then_inc(to_pe.sem, 1)

                @block.sync
                def _(sp):
                    for b in range(NB):
                        sp.wait_ge(to_pe.sem, b_cp + 3 * b + 3)
                        sp.dma_start(y_tab[b * P * NREL:(b + 1) * P * NREL, :].rearrange("(p r) o -> p (r o)", p=P),
                                     yb[:, b % 2, :]).then_inc(y_out[b % 2], 16)
                    sp.wait_ge(y_out[0], 16 * ((NB + 1) // 2))
                    sp.wait_ge(y_out[1], 16 * (NB // 2))
            dst_pass("msg", y_tab, rel_d, 17, agg)
            b_to, b_fr = to_act.base(1), from_act.base(1)
            with nc.Block() as block:
                @block.vector
                def _(dve):
                    v_chain(dve, dve.tensor_tensor(tmp[:, :, :], agg[:, :, 16:32], each(s3), ALU.mult))
                    v_chain(dve, dve.tensor_tensor(tmp[:, :, :], tmp[:, :, :], agg[:, :, 0:16], ALU.add))
                    v_chain(dve, dve.tensor_tensor(x[:, :, :], x[:, :, :], tmp[:, :, :], ALU.add))
                    layernorm(dve, b_fr)

                @block.scalar
                def _(act):
                    root_step(act, b_to)

        with ExitStack() as st:
            w1 = sb("rw1", [P, 32], F32, st)
            r1 = sb("rr1", [FIN, 32], F32, st)
            bb1 = sb("rb1", [32, 1], F32, st)
            w2_ = sb("rw2", [P, 2, 16], F32, st)
            r2 = sb("rr2", [32, 16], F32, st)
            bb2 = sb("rb2", [P, 16], F32, st)
            mT = sb("mT", [P, 2, NP], F32, st)
            h3T = sb("h3T", [32, NP], F32, st)
            h3 = sb("h3", [P, NB, 32], F32, st)
            mean = sb("mean", [P, NB, 256], F32, st)
            load([(w1[:, :], a["L3_gnn_W1"].rearrange("r i o -> (r i) o")), (r1[:, :], a["L3_gnn_root1"]),
                  (bb1[:, :], column(a["L3_gnn_b1"])),
                  (w2_[:, :, :], a["L3_gnn_W2"].rearrange("r i o -> (r i) o").rearrange("(c k) o -> k c o", c=2)),
                  (r2[:, :], a["L3_gnn_root2"]), (bb2[:, :], spread(a["L3_gnn_b2"], 16)),
                  (x_tab.rearrange("(b p) f -> p b f", p=P), x[:, :, :])])
            with ExitStack() as st2:
                agg = sb("agg3", [P, NB, 136], F32, st2)
                dst_pass("types", x_tab, src_d, 16, agg)
                with nc.Block() as block:
                    @block.vector
                    def _(dve):
                        v_chain(dve, dve.tensor_scalar(nrm_d[:, :, :], agg[:, :, 128:136], 1.0, None, ALU.max))
                        v_chain(dve, dve.reciprocal(nrm_d[:, :, :], nrm_d[:, :, :]))
                        for b in range(NB):
                            dve.tensor_tensor(mean[:, b, 0:128].rearrange("p (r f) -> p r f", r=NTYPE),
                                              agg[:, b, 0:128].rearrange("p (r f) -> p r f", r=NTYPE),
                                              nrm_d[:, b, :, None].to_broadcast([P, NTYPE, 16]), ALU.mult)
            turn_block(mean[:, :, 0:128], P, mT[:, 0, :])
            turn_block(x, FIN, xT)
            features([w1[:, :], r1[:, :]], [mT[:, 0, :], xT], h3T, 32, ACT.Relu, bb1[:, 0:1])
            b_mm, b_cp = from_pe.base(2), to_pe.base(1)
            with nc.Block() as block:
                @block.tensor
                def _(pe):
                    for b in range(NB):
                        m = pe.transpose(banks[b // 16][:, (b % 16) * 32:(b % 16 + 1) * 32], h3T[:, b * P:(b + 1) * P], ident[0:32, 0:32])
                        if b in (15, NB - 1):
                            m.then_inc(from_pe.sem, 1)

                @block.vector
                def _(dve):
                    dve.wait_ge(from_pe.sem, b_mm + 1)
                    dve.tensor_copy(h3[:, 0:16, :], banks[0][:, :].rearrange("p (b f) -> p b f", f=32))
                    dve.wait_ge(from_pe.sem, b_mm + 2)
                    dve.tensor_copy(h3[:, 16:NB, :], banks[1][:, 0:(NB - 16) * 32].rearrange("p (b f) -> p b f", f=32)).then_inc(to_pe.sem, 1)
            save([(h3_tab.rearrange("(b p) f -> p b f", p=P), h3[:, :, :])])
            dst_pass("types_only", h3_tab, src_d, 32, mean)
            with nc.Block() as block:
                @block.vector
                def _(dve):
                    for b in range(NB):
                        v = mean[:, b, :].rearrange("p (r f) -> p r f", r=NTYPE)
                        dve.tensor_tensor(v, v, nrm_d[:, b, :, None].to_broadcast([P, NTYPE, 32]), ALU.mult)
            turn_block(mean[:, :, 0:128], P, mT[:, 0, :])
            turn_block(mean[:, :, 128:256], P, mT[:, 1, :])
            nodes([(mT[:, 0, :], w2_[:, 0, :]), (mT[:, 1, :], w2_[:, 1, :]), (h3T, r2[:, :])], FIN, 0)
            b_to, b_fr = to_act.base(1), from_act.base(1)
            with nc.Block() as block:
                @block.vector
                def _(dve):
                    o = banks[0][:, 0:NB * FIN].rearrange("p (b f) -> p b f", b=NB)
                    v_chain(dve, dve.tensor_tensor(tmp[:, :, :], o, row(bb2), ALU.add))
                    v_chain(dve, dve.tensor_tensor(x[:, :, :], x[:, :, :], tmp[:, :, :], ALU.add))
                    layernorm(dve, b_fr)

                @block.scalar
                def _(act):
                    root_step(act, b_to)
            full = (N // P) * P
            save([(out[0:full, :].rearrange("(b p) f -> p b f", p=P), x[:, 0:N // P, :]),
                  (out[full:N, :], x[0:N - full, NB - 1, :])])


def kernel(**inputs):
    import numpy as _np
    import concourse.bacc as _bacc
    from concourse import mybir as _mybir
    from concourse.bass_utils import run_bass_kernel_spmd as _run

    nc = _bacc.Bacc("TRN2", target_bir_lowering=False, num_devices=1)
    arrays, args = {}, {}
    for name, v in inputs.items():
        v = _np.ascontiguousarray(v)
        if v.ndim == 0:
            v = v.reshape(1, 1)
        arrays[f"in_{name}_dram"] = v
        args[name] = nc.dram_tensor(f"in_{name}_dram", v.shape, _mybir.dt.from_np(v.dtype), kind="ExternalInput").ap()
    out = nc.dram_tensor("out_0_dram", (N, FIN), F32, kind="ExternalOutput").ap()
    gnn_kernel(nc, args, out)
    r = _run(nc, [arrays], core_ids=[0])
    return r.results[0]["out_0_dram"]
```
